# Optimizing a Trainium2 kernel written in Bass

```python
import numpy as np
import jax
import jax.numpy as jnp

def _softmax(x, axis=-1):
    return jax.nn.softmax(x, axis=axis)

def _gelu(x):
    return jax.nn.gelu(x, approximate=True)

def _silu(x):
    return jax.nn.silu(x)

def _sigmoid(x):
    return jax.nn.sigmoid(x)

def _layernorm(x, axis=-1, eps=1e-05):
    m = jnp.mean(x, axis=axis, keepdims=True)
    v = jnp.var(x, axis=axis, keepdims=True)
    return (x - m) / jnp.sqrt(v + eps)

def _scatter_add(tgt, idx, src, axis=0):
    return tgt.at[idx].add(src)

def _segment_sum(src, seg, n):
    return jax.ops.segment_sum(src, seg, n)
kernel_name = 'mk_macaron_d1_jaxref_r8_708acc'

def setup_inputs(seed: int=0):
    np.random.seed(seed)
    _w = jnp.asarray

    def _L0_attn_setup():
        import jax, jax.numpy as jnp
        import numpy as np
        HIDDEN = 128
        BATCH = 4
        SEQ = 256

        def _dense(key, din, dout):
            kw, _ = jax.random.split(key)
            W = jax.random.normal(kw, (din, dout), dtype=jnp.float32) * 0.02
            b = jnp.zeros((dout,), dtype=jnp.float32)
            return (W, b)

        def _forward(x, Wg, bg, Wi, bi, A, Bp, Cp, Dp, gamma, beta, Wfg, bfg, Wfu, bfu, Wfd, bfd, Wo, bo):
            B, T, D = x.shape
            silu = jax.nn.silu
            gate = silu(x @ Wg + bg)
            u = gate * (x @ Wi + bi)
            t = jnp.arange(T, dtype=jnp.float32)[:, None]
            kernel = Bp * jnp.power(A[None, :], t)
            fft_len = 1 << int(np.ceil(np.log2(2 * T - 1)))
            Uf = jnp.fft.rfft(u, n=fft_len, axis=1)
            Kf = jnp.fft.rfft(kernel, n=fft_len, axis=0)
            y = jnp.fft.irfft(Uf * Kf[None], n=fft_len, axis=1)[:, :T, :]
            y = Cp * y + Dp * u
            mu = jnp.mean(y, axis=-1, keepdims=True)
            var = jnp.mean(jnp.square(y - mu), axis=-1, keepdims=True)
            y = (y - mu) * jax.lax.rsqrt(var + 0.001) * gamma + beta
            y = silu(y @ Wfg + bfg) * (y @ Wfu + bfu) @ Wfd + bfd
            return y @ Wo + bo
        key = jax.random.key(seed)
        ks = jax.random.split(key, 12)
        D = HIDDEN
        x = jax.random.normal(ks[0], (BATCH, SEQ, D), dtype=jnp.float32)
        Wg, bg = _dense(ks[1], D, D)
        Wi, bi = _dense(ks[2], D, D)
        A = -0.5 + 0.1 * jax.random.normal(ks[3], (D,), dtype=jnp.float32)
        Bp = 0.05 * jax.random.normal(ks[4], (D,), dtype=jnp.float32)
        Cp = 0.05 * jax.random.normal(ks[5], (D,), dtype=jnp.float32)
        Dp = jnp.zeros((D,), dtype=jnp.float32)
        gamma = jnp.ones((D,), dtype=jnp.float32)
        beta = jnp.zeros((D,), dtype=jnp.float32)
        Wfg, bfg = _dense(ks[6], D, D)
        Wfu, bfu = _dense(ks[7], D, D)
        Wfd, bfd = _dense(ks[8], D, D)
        Wo, bo = _dense(ks[9], D, D)
        return {'x': x, 'Wg': Wg, 'bg': bg, 'Wi': Wi, 'bi': bi, 'A': A, 'Bp': Bp, 'Cp': Cp, 'Dp': Dp, 'gamma': gamma, 'beta': beta, 'Wfg': Wfg, 'bfg': bfg, 'Wfu': Wfu, 'bfu': bfu, 'Wfd': Wfd, 'bfd': bfd, 'Wo': Wo, 'bo': bo}
    _L0_attn_in = _L0_attn_setup()

    def _L0_ffn_setup():
        import jax, jax.numpy as jnp
        import numpy as np
        D = 128
        H = 512
        E = 12
        K = 3
        B, S = (1, 256)
        key = jax.random.key(seed)
        ks = jax.random.split(key, 6)
        scale = 0.02
        x = jax.random.normal(ks[0], (B, S, D), dtype=jnp.float32)
        Wg = jax.random.normal(ks[1], (D, E), dtype=jnp.float32) * scale
        Wup = jax.random.normal(ks[2], (E, D, H), dtype=jnp.float32) * scale
        bup = jax.random.normal(ks[3], (E, H), dtype=jnp.float32) * scale
        Wdown = jax.random.normal(ks[4], (E, H, D), dtype=jnp.float32) * scale
        bdown = jax.random.normal(ks[5], (E, D), dtype=jnp.float32) * scale
        return {'x': x, 'Wg': Wg, 'Wup': Wup, 'bup': bup, 'Wdown': Wdown, 'bdown': bdown}
    _L0_ffn_in = _L0_ffn_setup()
    _d = {'L0_attn_x': _L0_attn_in['x'], 'L0_attn_Wg': _L0_attn_in['Wg'], 'L0_attn_bg': _L0_attn_in['bg'], 'L0_attn_Wi': _L0_attn_in['Wi'], 'L0_attn_bi': _L0_attn_in['bi'], 'L0_attn_A': _L0_attn_in['A'], 'L0_attn_Bp': _L0_attn_in['Bp'], 'L0_attn_Cp': _L0_attn_in['Cp'], 'L0_attn_Dp': _L0_attn_in['Dp'], 'L0_attn_gamma': _L0_attn_in['gamma'], 'L0_attn_beta': _L0_attn_in['beta'], 'L0_attn_Wfg': _L0_attn_in['Wfg'], 'L0_attn_bfg': _L0_attn_in['bfg'], 'L0_attn_Wfu': _L0_attn_in['Wfu'], 'L0_attn_bfu': _L0_attn_in['bfu'], 'L0_attn_Wfd': _L0_attn_in['Wfd'], 'L0_attn_bfd': _L0_attn_in['bfd'], 'L0_attn_Wo': _L0_attn_in['Wo'], 'L0_attn_bo': _L0_attn_in['bo'], 'L0_ffn_Wg': _L0_ffn_in['Wg'], 'L0_ffn_Wup': _L0_ffn_in['Wup'], 'L0_ffn_bup': _L0_ffn_in['bup'], 'L0_ffn_Wdown': _L0_ffn_in['Wdown'], 'L0_ffn_bdown': _L0_ffn_in['bdown']}
    _x0 = _d['L0_attn_x']
    _d['L0_attn_x'] = jax.random.normal(jax.random.fold_in(jax.random.key(seed), 1), (8, 512, 128), dtype=_x0.dtype)
    del _x0
    return _d

def reference(L0_attn_x, L0_attn_Wg, L0_attn_bg, L0_attn_Wi, L0_attn_bi, L0_attn_A, L0_attn_Bp, L0_attn_Cp, L0_attn_Dp, L0_attn_gamma, L0_attn_beta, L0_attn_Wfg, L0_attn_bfg, L0_attn_Wfu, L0_attn_bfu, L0_attn_Wfd, L0_attn_bfd, L0_attn_Wo, L0_attn_bo, L0_ffn_Wg, L0_ffn_Wup, L0_ffn_bup, L0_ffn_Wdown, L0_ffn_bdown):

    def _L0_attn_ref(x, Wg, bg, Wi, bi, A, Bp, Cp, Dp, gamma, beta, Wfg, bfg, Wfu, bfu, Wfd, bfd, Wo, bo):
        import jax, jax.numpy as jnp
        import numpy as np
        HIDDEN = 128
        BATCH = 4
        SEQ = 256

        def _dense(key, din, dout):
            kw, _ = jax.random.split(key)
            W = jax.random.normal(kw, (din, dout), dtype=jnp.float32) * 0.02
            b = jnp.zeros((dout,), dtype=jnp.float32)
            return (W, b)

        def _forward(x, Wg, bg, Wi, bi, A, Bp, Cp, Dp, gamma, beta, Wfg, bfg, Wfu, bfu, Wfd, bfd, Wo, bo):
            B, T, D = x.shape
            silu = jax.nn.silu
            gate = silu(x @ Wg + bg)
            u = gate * (x @ Wi + bi)
            t = jnp.arange(T, dtype=jnp.float32)[:, None]
            kernel = Bp * jnp.power(A[None, :], t)
            fft_len = 1 << int(np.ceil(np.log2(2 * T - 1)))
            Uf = jnp.fft.rfft(u, n=fft_len, axis=1)
            Kf = jnp.fft.rfft(kernel, n=fft_len, axis=0)
            y = jnp.fft.irfft(Uf * Kf[None], n=fft_len, axis=1)[:, :T, :]
            y = Cp * y + Dp * u
            mu = jnp.mean(y, axis=-1, keepdims=True)
            var = jnp.mean(jnp.square(y - mu), axis=-1, keepdims=True)
            y = (y - mu) * jax.lax.rsqrt(var + 0.001) * gamma + beta
            y = silu(y @ Wfg + bfg) * (y @ Wfu + bfu) @ Wfd + bfd
            return y @ Wo + bo
        return _forward(x, Wg, bg, Wi, bi, A, Bp, Cp, Dp, gamma, beta, Wfg, bfg, Wfu, bfu, Wfd, bfd, Wo, bo)

    def _L0_ffn_ref(x, Wg, Wup, bup, Wdown, bdown):
        import jax, jax.numpy as jnp
        import numpy as np
        D = 128
        H = 512
        E = 12
        K = 3
        B, S = (1, 256)
        gate_logits = jnp.einsum('bsd,de->bse', x, Wg)
        topw, sel = jax.lax.top_k(gate_logits, K)
        topw = jax.nn.softmax(topw.astype(jnp.float32), axis=-1).astype(x.dtype)
        cw = jnp.einsum('bsk,bske->bse', topw, jax.nn.one_hot(sel, E, dtype=x.dtype))
        h = jax.nn.gelu(jnp.einsum('bsd,edh->ebsh', x, Wup) + bup[:, None, None, :], approximate=False)
        y = jnp.einsum('ebsh,ehd->ebsd', h, Wdown) + bdown[:, None, None, :]
        return jnp.einsum('bse,ebsd->bsd', cw, y)
    x = L0_attn_x
    x = x + 0.5 * _L0_ffn_ref(_layernorm(x, axis=-1), L0_ffn_Wg, L0_ffn_Wup, L0_ffn_bup, L0_ffn_Wdown, L0_ffn_bdown)
    x = x + _L0_attn_ref(_layernorm(x, axis=-1), L0_attn_Wg, L0_attn_bg, L0_attn_Wi, L0_attn_bi, L0_attn_A, L0_attn_Bp, L0_attn_Cp, L0_attn_Dp, L0_attn_gamma, L0_attn_beta, L0_attn_Wfg, L0_attn_bfg, L0_attn_Wfu, L0_attn_bfu, L0_attn_Wfd, L0_attn_bfd, L0_attn_Wo, L0_attn_bo)
    x = x + 0.5 * _L0_ffn_ref(_layernorm(x, axis=-1), L0_ffn_Wg, L0_ffn_Wup, L0_ffn_bup, L0_ffn_Wdown, L0_ffn_bdown)
    return x

_drawn_inputs = setup_inputs


def setup_inputs(seed=0):
    import zlib

    import numpy as np

    out = dict(_drawn_inputs(seed))
    spreads = {'L0_attn_bg': (0.0, 0.1),
     'L0_attn_bi': (0.0, 0.1),
     'L0_attn_Dp': (0.0, 0.1),
     'L0_attn_gamma': (1.0, 0.2),
     'L0_attn_beta': (0.0, 0.1),
     'L0_attn_bfg': (0.0, 0.1),
     'L0_attn_bfu': (0.0, 0.1),
     'L0_attn_bfd': (0.0, 0.1),
     'L0_attn_bo': (0.0, 0.1)}
    factors = {}
    for name, (base, spread) in spreads.items():
        noise = np.random.default_rng([zlib.crc32(name.encode()), seed]).standard_normal(out[name].shape)
        drawn = base * np.exp(spread * noise) if base else spread * noise
        out[name] = jnp.asarray(drawn.astype(out[name].dtype))
    for name, factor in factors.items():
        out[name] = (out[name] * factor).astype(out[name].dtype)
    return out
```

```python
from contextlib import ExitStack

import concourse.bass as bass
from concourse import mybir

F32 = mybir.dt.float32
BF16 = mybir.dt.bfloat16
U32 = mybir.dt.uint32
I32 = mybir.dt.int32
ALU = mybir.AluOpType
ACT = mybir.ActivationFunctionType
AX = mybir.AxisListType

P = 128
D = 128
HID = 512
E = 12
K = 3
T = 4096
NH = 2
NT = T // P // NH
NQ = NT // 4
NTL = (K * NT * P + E * (P - 1)) // P
NG = (NTL + 3) // 4
RSQRT_SEED = float(0x5F3759DF)


class Queues:

    def __init__(self, sems):
        self.sem = sems
        self.q = {e: [] for e in sems}
        self.n = {e: 0 for e in sems}
        self.landed = {}

    def op(self, e, fn, *waits):
        self.n[e] += 1
        self.q[e].append((waits, fn, self.sem[e], 1))
        return self.sem[e], self.n[e]

    def dma(self, e, fn, sem, *waits):
        self.landed[sem.name] = self.landed.get(sem.name, 0) + 16
        self.q[e].append((waits, fn, sem, 16))
        return sem, self.landed[sem.name]

    def wait(self, e, *waits):
        self.q[e].append((waits, None, None, 0))

    def emit(self, e, eng):
        seen = {}
        for waits, fn, sem, by in self.q[e]:
            for s, v in waits:
                if seen.get(s.name, 0) < v:
                    eng.wait_ge(s, v)
                    seen[s.name] = v
            if fn is not None:
                fn(eng).then_inc(sem, by)


def macaron_kernel(nc, a, out):
    with ExitStack() as ctx:
        def sb(name, shape, dt=F32):
            return ctx.enter_context(nc.sbuf_tensor(name, shape, dt))

        def sem(name):
            return ctx.enter_context(nc.semaphore(name))

        psum = [ctx.enter_context(nc.psum_tensor(f"ps{i}", [P, 512], F32)) for i in range(8)]

        xs = [nc.dram_tensor(f"xs{h}", [NTL * P, D], F32, kind="Internal").ap() for h in range(NH)]
        ys = [nc.dram_tensor(f"ys{h}", [NTL * P, D], F32, kind="Internal").ap() for h in range(NH)]

        W = sb("W", [P, E, 2 * HID])
        bupB = sb("bupB", [P, E, HID])
        bdB = sb("bdB", [P, E, D])
        X = sb("X", [P, NH * NT, D])
        XN = [sb(f"XN{h}", [P, NT, D]) for h in range(NH)]
        wgate = sb("wgate", [P, E])
        wat = {n: sb("w_" + n, [P, D]) for n in ("Wg", "Wi", "Wfg", "Wfu", "Wfd", "Wo")}
        vec = {n: sb("v_" + n, [P, 1]) for n in
               ("bg", "bi", "A", "Bp", "Cp", "Dp", "gamma", "beta", "bfg", "bfu", "bfd")}
        bgh, bfgh, cB, cD, bc = (sb(n, [P, 1]) for n in ("bgh", "bfgh", "cB", "cD", "bc"))
        boB = sb("boB", [P, D])
        Arep = sb("Arep", [P, 512])
        ident = sb("ident", [P, P])
        LT = sb("LT", [P, P], BF16)
        ones = sb("ones", [P, P], BF16)
        io12i, io12 = sb("io12i", [P, E], I32), sb("io12", [P, E])
        ioci, ioc = sb("ioci", [P, NT], I32), sb("ioc", [P, NT])
        iotli, iotl = sb("iotli", [1, NTL], I32), sb("iotl", [1, NTL])
        rmask = sb("rmask", [P, E, NT])
        one12 = sb("one12", [P, E])

        L = sb("L", [P, NT, E])
        V = sb("V", [P, NT, 8])
        IX = sb("IX", [P, NT, 8], U32)
        IF = sb("IF", [P, NT, K])
        dV, eV = sb("dV", [P, NT, K]), sb("eV", [P, NT, K])
        sV, rV = sb("sV", [P, NT]), sb("rV", [P, NT])
        WK = [sb(f"WK{h}", [P, NT, K]) for h in range(NH)]
        OH = sb("OH", [P, K, NT, E])
        M01, M = sb("M01", [P, NT, E]), sb("M", [P, NT, E], BF16)
        tot, cum, excl, gt = (sb(n, [P, E, NT]) for n in ("tot", "cum", "excl", "gt"))
        nte, end, base = (sb(n, [P, E]) for n in ("nte", "end", "base"))
        SL, SL2 = sb("SL", [P, E, NT]), sb("SL2", [P, NT, E])
        tk = sb("tk", [P, K, NT, E])
        SLF = sb("SLF", [P, K, NT])
        SLU = [sb(f"SLU{h}", [P, K, NT], U32) for h in range(NH)]
        ge = sb("ge", [1, NTL, E])
        EF, EM = sb("EF", [1, NTL]), sb("EM", [1, NTL])
        eoff = [{n: sb(f"eoff{h}_{n}", [1, NTL], U32) for n in (1024, 512, 128)} for h in range(NH)]

        xl = [sb(f"xl{i}", [P, 4, D]) for i in range(2)]
        xT = [sb(f"xT{i}", [P, 512]) for i in range(2)]
        Hb = [sb(f"Hb{i}", [P, 512]) for i in range(2)]
        G = [sb(f"G{i}", [P, 512]) for i in range(2)]
        hT = [sb(f"hT{i}", [P, 512]) for i in range(2)]
        Ys = [sb(f"Ys{i}", [P, 4, D]) for i in range(2)]
        NYG = 12
        YG = sb("YG", [P, NYG, D])

        st6, mv = sb("st6", [P, 4, 6]), sb("mv", [P, 4, 2])
        v1, nr, na, nb = (sb(n, [P, 4]) for n in ("v1", "nr", "na", "nb"))
        xr = sb("xr", [P, 4, D])
        sT = sb("sT", [P, 512])
        tg, ag, bu, u2, sc, wv, yv = (sb(n, [P, 512]) for n in ("tg", "ag", "bu", "u2", "sc", "wv", "yv"))
        zero = sb("zero", [P, 4 * D])

        s_eng = {e: sem("s_" + e) for e in ("pe", "dve", "act", "pool")}
        Q = Queues({**s_eng, "sp": s_eng["pe"]})
        op, dma = Q.op, Q.dma
        s_x = [sem(f"s_x{i}") for i in range(8)]
        s_w, s_wl, s_v = sem("s_w"), sem("s_wl"), sem("s_v")
        s_z = [sem(f"s_z{h}") for h in range(NH)]
        s_xl = [sem(f"s_xl{i}") for i in range(2)]
        s_ys = [sem(f"s_ys{i}") for i in range(2)]
        s_sc = [sem(f"s_sc{h}") for h in range(NH)]
        s_yg = [sem(f"s_yg{i}") for i in range(NYG)]
        s_out = sem("s_out")

        xv = a["x"].rearrange("b s d -> (b s) d").rearrange("(t p) d -> p t d", p=P)
        ov = out.rearrange("b s d -> (b s) d").rearrange("(t p) d -> p t d", p=P)
        t_x = {}
        for q in range(NH * NQ):
            t_x[q] = dma("sp", lambda e, q=q: e.dma_start(X[:, 4 * q:4 * q + 4, :], xv[:, 4 * q:4 * q + 4, :]), s_x[q])
            if q == 0:
                t_wg = dma("sp", lambda e: e.dma_start(wgate[:], a["ffn_Wg"]), s_v)
        for n in vec:
            t_v = dma("sp", lambda e, n=n: e.dma_start(vec[n][:], a["attn_" + n].rearrange("(p o) -> p o", o=1)), s_v)
        for n in wat:
            t_v = dma("sp", lambda e, n=n: e.dma_start(wat[n][:], a["attn_" + n]), s_v)
        t_v = dma("sp", lambda e: e.dma_start(boB[:], a["attn_bo"].rearrange("(o d) -> o d", o=1).to_broadcast([P, D])), s_v)

        t_zero = op("dve", lambda e: e.memset(zero[:], 0.0))
        zrows = zero[:, :].rearrange("p (r d) -> p r d", d=D)
        t_z = [None] * NH
        for h in range(NH):
            zv = xs[h].rearrange("(p r) d -> p r d", p=P)
            for r in range(0, NTL, 4):
                n = min(4, NTL - r)
                t_z[h] = dma("act", lambda e, zv=zv, r=r, n=n: e.dma_start(zv[:, r:r + n, :], zrows[:, 0:n, :]),
                             s_z[h], t_zero)
        for e0 in range(0, E, 4):
            t_w = dma("sp", lambda e, e0=e0: e.dma_start(
                W[:, e0:e0 + 4, 0:HID], a["ffn_Wup"][e0:e0 + 4].rearrange("e p h -> p e h")), s_w)
            t_bu = dma("sp", lambda e, e0=e0: e.dma_start(
                bupB[:, e0:e0 + 4, :].rearrange("p e h -> p (e h)"),
                a["ffn_bup"][e0:e0 + 4].rearrange("e h -> (e h)").rearrange("(o n) -> o n", o=1).to_broadcast([P, 4 * HID])), s_w)
            for x0 in range(e0, e0 + 4):
                t_w = dma("sp", lambda e, x0=x0: e.dma_start(
                    W[:, x0, HID:2 * HID].rearrange("p (c d) -> p c d", d=D),
                    a["ffn_Wdown"][x0].rearrange("(c p) d -> p c d", p=P)), s_w)
        t_w = dma("sp", lambda e: e.dma_start(
            bdB[:, :, :].rearrange("p e d -> p (e d)"),
            a["ffn_bdown"].rearrange("e d -> (e d)").rearrange("(o n) -> o n", o=1).to_broadcast([P, E * D])), s_w)

        t = op("pool", lambda e: e.memset(ident[:], 0.0))
        t_id = op("pool", lambda e: e.affine_select(out=ident[:], in_=ident[:], compare_op=ALU.not_equal, fill=1.0,
                                                    base=0, pattern=[[-1, P]], channel_multiplier=1), t)
        t = op("pool", lambda e: e.memset(LT[:], 1.0))
        t_lt = op("pool", lambda e: e.affine_select(out=LT[:], in_=LT[:], compare_op=ALU.is_gt, fill=0.0,
                                                    base=0, pattern=[[1, P]], channel_multiplier=-1), t)
        op("pool", lambda e: e.memset(ones[:], 1.0))
        op("pool", lambda e: e.iota(io12i[:], [[1, E]], base=0, channel_multiplier=0))
        op("pool", lambda e: e.iota(ioci[:], [[P, NT]], base=0, channel_multiplier=0))
        t = op("pool", lambda e: e.iota(iotli[:], [[1, NTL]], base=0, channel_multiplier=0))
        op("dve", lambda e: e.tensor_copy(io12[:], io12i[:]), t)
        op("dve", lambda e: e.tensor_copy(ioc[:], ioci[:]))
        op("dve", lambda e: e.tensor_copy(iotl[:], iotli[:]))
        op("dve", lambda e: e.memset(one12[:], 1.0))
        t = op("dve", lambda e: e.memset(rmask[:], 1.0))
        t_cst = op("dve", lambda e: e.memset(rmask[:, :, 0:1], 0.0), t)
        t_const = op("pool", lambda e: e.tensor_copy(ioci[:], ioci[:]), t_cst)

        def attn_consts():
            op("dve", lambda e: e.tensor_scalar(bgh[:], vec["bg"][:], 0.5, None, ALU.mult), t_v)
            op("dve", lambda e: e.tensor_scalar(bfgh[:], vec["bfg"][:], 0.5, None, ALU.mult))
            op("dve", lambda e: e.tensor_scalar(cD[:], vec["Dp"][:], 0.5, None, ALU.mult))
            t = op("dve", lambda e: e.tensor_tensor(bc[:], vec["Bp"][:], vec["Cp"][:], ALU.mult))
            op("dve", lambda e: e.tensor_scalar(cB[:], bc[:], 0.5, None, ALU.mult), t)
            t = op("dve", lambda e: e.memset(Arep[:], 0.0))
            return op("dve", lambda e: e.tensor_scalar(Arep[:], Arep[:], vec["A"][:, 0:1], None, ALU.add), t)

        side_banks = [psum[6], psum[7]]
        bank_free = [[], []]
        turn = [0]

        def bank():
            b = turn[0] % 2
            turn[0] += 1
            return b, side_banks[b], bank_free[b]

        tok = {"X": {}, "XN": [[], []], "sT": [], "xr": [], "L": [], "route": [], "att": [],
               "eoff": [[], []], "SLU": [[], []], "WK": [[], []]}

        def norm_rows(src, dst, eps, ready, dst_free):
            def stats(e):
                for j in range(4):
                    i = e.bn_stats(st6[:, j, :], src[j])
                return i

            def aggr(e):
                for j in range(4):
                    i = e.bn_aggr(mv[:, j, :], st6[:, j, :])
                return i
            t = op("dve", stats, *ready)
            t = op("dve", aggr, t)
            t = op("dve", lambda e: e.tensor_scalar(v1[:], mv[:, :, 1], eps, None, ALU.add), t)
            t = op("dve", lambda e: e.tensor_scalar(na[:].bitcast(U32), v1[:].bitcast(U32), 1, None,
                                                    ALU.logical_shift_right), t)
            t = op("dve", lambda e: e.tensor_scalar(nr[:].bitcast(I32), na[:].bitcast(I32), -1.0, RSQRT_SEED,
                                                    ALU.mult, ALU.add), t)
            for _ in range(3):
                t = op("dve", lambda e: e.tensor_tensor(na[:], nr[:], nr[:], ALU.mult), t)
                t = op("dve", lambda e: e.scalar_tensor_tensor(nb[:], na[:], -0.5, v1[:], ALU.mult, ALU.mult), t)
                t = op("dve", lambda e: e.scalar_tensor_tensor(nr[:], nb[:], 1.5, nr[:], ALU.add, ALU.mult), t)

            def scale(e):
                for j in range(4):
                    i = e.tensor_scalar(dst[j], src[j], mv[:, j, 0:1], nr[:, j:j + 1], ALU.subtract, ALU.mult)
                return i
            return op("dve", scale, t, *dst_free)

        def turn4(src, ready):
            b, ps, free = bank()

            def go(e):
                for j in range(4):
                    i = e.transpose(ps[:, j * P:(j + 1) * P], src[j], ident[:])
                return i
            return b, ps, op("pe", go, t_id, *ready, *free)

        def side_mm(w, rhs, ready):
            b, ps, free = bank()
            return b, ps, op("pe", lambda e: e.matmul(ps[:], w[:], rhs[:], start=True, stop=True), *ready, *free)

        def route_quad(h, q):
            g = h * NQ + q
            src = [X[:, 4 * g + j, :] for j in range(4)]
            dst = [XN[h][:, 4 * q + j, :] for j in range(4)]
            t = norm_rows(src, dst, 1e-5, tok["X"].get(g, [t_x[g]]), tok["XN"][h])
            tok[("xn", h, q)] = t
            yield
            b, ps, tt = turn4(dst, [t])
            tc = op("act", lambda e, ps=ps: e.activation(sT[:], ps[:], ACT.Copy), tt, *tok["sT"])
            bank_free[b] = [tc]
            yield
            b, ps, free = bank()

            def logits(e):
                for j in range(4):
                    i = e.matmul(ps[:, j * E:(j + 1) * E], sT[:, j * P:(j + 1) * P], wgate[:], start=True, stop=True)
                return i
            tl = op("pe", logits, tc, t_wg, t_v, *free)
            tok["sT"] = [tl]
            tok["Lq"] = op("dve", lambda e: e.tensor_copy(
                L[:, 4 * q:4 * q + 4, :], ps[:, 0:4 * E].rearrange("p (t e) -> p t e", e=E)), tl, *tok["route"])
            bank_free[b] = [tok["Lq"]]
            yield

        def route_tail(h):
            def maxes(e):
                for t in range(NT):
                    i = e.max(V[:, t, :], L[:, t, :])
                return i

            def idxs(e):
                for t in range(NT):
                    i = e.max_index(IX[:, t, :], V[:, t, :], L[:, t, :])
                return i
            t = op("dve", maxes, tok["Lq"], *tok["route"])
            td = op("dve", lambda e: e.tensor_tensor(dV[:], V[:, :, 0:K], V[:, :, 0:1].to_broadcast([P, NT, K]),
                                                     ALU.subtract), t)
            te = op("act", lambda e: e.activation(eV[:], dV[:], ACT.Exp), td)
            t = op("dve", idxs, t)
            yield
            t = op("dve", lambda e: e.tensor_copy(IF[:], IX[:, :, 0:K]), t)

            def hot(e):
                for k in range(K):
                    i = e.tensor_tensor(OH[:, k, :, :], IF[:, :, k:k + 1].to_broadcast([P, NT, E]),
                                        io12[:, :].rearrange("p (o e) -> p o e", o=1).to_broadcast([P, NT, E]),
                                        ALU.is_equal)
                return i
            t = op("dve", hot, t, t_cst)
            t = op("dve", lambda e: e.tensor_tensor(M01[:], OH[:, 0], OH[:, 1], ALU.add), t)
            t = op("dve", lambda e: e.tensor_tensor(M[:], M01[:], OH[:, 2], ALU.add), t)
            b, ps, free = bank()
            n = NT * E

            def count(e):
                mf = M[:, :, :].rearrange("p t e -> p (t e)")
                e.matmul(ps[:, 0:n], LT[:], mf, start=True, stop=True)
                return e.matmul(ps[:, n:2 * n], ones[:], mf, start=True, stop=True)
            tp = op("pe", count, t, t_const, *free)
            yield
            ts = op("dve", lambda e: e.tensor_reduce(sV[:], eV[:], AX.X, ALU.add), te)
            ts = op("dve", lambda e: e.reciprocal(rV[:], sV[:]), ts)
            tok["WK"][h] = [op("dve", lambda e: e.scalar_tensor_tensor(
                WK[h][:], eV[:], 0.5, rV[:, :].rearrange("p (t o) -> p t o", o=1).to_broadcast([P, NT, K]),
                ALU.mult, ALU.mult), ts, *tok["WK"][h])]
            t = op("dve", lambda e: e.tensor_copy(tot[:], ps[:, n:2 * n].rearrange("p (t e) -> p e t", e=E)), tp)

            def flat(x):
                return x[:, :, :].rearrange("p e t -> p (e t)")
            t = op("dve", lambda e: e.tensor_tensor_scan(flat(cum), flat(rmask), flat(tot), 0.0, ALU.mult, ALU.add), t)
            op("dve", lambda e: e.tensor_tensor(excl[:], cum[:], tot[:], ALU.subtract), t)
            t = op("dve", lambda e: e.tensor_tensor(
                gt[:], cum[:, :, NT - 1:NT].to_broadcast([P, E, NT]),
                ioc[:, :].rearrange("p (o t) -> p o t", o=1).to_broadcast([P, E, NT]), ALU.is_gt), t)
            t = op("dve", lambda e: e.tensor_reduce(nte[:], gt[:], AX.X, ALU.add), t)
            t = op("dve", lambda e: e.tensor_tensor_scan(end[:], one12[:], nte[:], 0.0, ALU.mult, ALU.add), t)
            t1 = op("dve", lambda e: e.tensor_tensor(base[:], end[:], nte[:], ALU.subtract), t)
            t = op("dve", lambda e: e.scalar_tensor_tensor(
                SL[:], base[:, :].rearrange("p (e o) -> p e o", o=1).to_broadcast([P, E, NT]), float(P), excl[:],
                ALU.mult, ALU.add), t1)
            t = op("dve", lambda e: e.tensor_tensor(
                SL2[:], ps[:, 0:n].rearrange("p (t e) -> p t e", e=E), SL[:, :, :].rearrange("p e t -> p t e"),
                ALU.add), t)
            bank_free[b] = [t]

            def pick(e):
                for k in range(K):
                    i = e.tensor_tensor(tk[:, k], OH[:, k], SL2[:], ALU.mult)
                return i
            t = op("dve", pick, t)
            t = op("dve", lambda e: e.tensor_reduce(SLF[:], tk[:], AX.X, ALU.add), t)
            tok["SLU"][h] = [op("dve", lambda e: e.tensor_copy(SLU[h][:], SLF[:]), t, *tok["SLU"][h])]
            yield
            t = op("dve", lambda e: e.tensor_tensor(
                ge[:], iotl[:, :].rearrange("p (i o) -> p i o", o=1).to_broadcast([1, NTL, E]),
                end[0:1, :].rearrange("p (o e) -> p o e", o=1).to_broadcast([1, NTL, E]), ALU.is_ge), t1)
            t = op("dve", lambda e: e.tensor_reduce(EF[:], ge[:], AX.X, ALU.add), t)
            t = op("dve", lambda e: e.tensor_scalar(EM[:], EF[:], float(E - 1), None, ALU.min), t)

            def offsets(e):
                for n in (1024, 512, 128):
                    i = e.tensor_scalar(eoff[h][n][:], EM[:], float(n), None, ALU.mult)
                return i
            tok["eoff"][h] = [op("dve", offsets, t, *tok["eoff"][h])]
            tok["route"] = tok["eoff"][h]
            yield

        def scatter(h):
            for t in range(NT):
                for k in range(K):
                    last = dma("pool", lambda e, t=t, k=k: e.indirect_dma_start(
                        xs[h], bass.IndirectOffsetOnAxis(SLU[h][:, k, t:t + 1], 0), XN[h][:, t, :], None,
                        bounds_check=NTL * P - 1, oob_is_err=False),
                        s_sc[h], t_z[h], *tok["SLU"][h], tok[("xn", h, NQ - 1)], *tok.get(("xl", h), []))
            tok["XN"][h] = [last]
            tok[("sc", h)] = [last]

        xl_free, xT_free, Hb_free, G_free, hT_free = ([[], []] for _ in range(5))
        H_free, HT_free, Ys_free = [[], []], [[], []], [[], []]
        XT_free, Y_free = [], []
        xT_ready = [None, None]

        def ffn(h):
            HB, HTB, XTB, YB = psum[0:2], psum[2:4], psum[4], psum[5]
            W2 = W[:, :, :].rearrange("p e n -> p (e n)")
            BU = bupB[:, :, :].rearrange("p e n -> p (e n)")
            BD = bdB[:, :, :].rearrange("p e n -> p (e n)")
            xsv = xs[h].rearrange("(t p) d -> p t d", p=P)
            ysv = ys[h].rearrange("(t p) d -> p t d", p=P)
            t_load = {}

            def size(g):
                return min(4, NTL - 4 * g)

            def load(g):
                n = size(g)
                t_load[g] = dma("sp", lambda e: e.dma_start(xl[g % 2][:, 0:n, :], xsv[:, 4 * g:4 * g + n, :]),
                                s_xl[g % 2], *tok[("sc", h)], *xl_free[g % 2])

            def turn_x(g):
                n = size(g)

                def go(e):
                    for j in range(n):
                        i = e.transpose(XTB[:, j * P:(j + 1) * P], xl[g % 2][:, j, :], ident[:])
                    return i
                t = op("pe", go, t_load[g], *XT_free)
                xl_free[g % 2] = [t]
                t = op("act", lambda e: e.activation(xT[g % 2][:, 0:n * P], XTB[:, 0:n * P], ACT.Copy), t, *xT_free[g % 2])
                XT_free[:] = [t]
                xT_ready[g % 2] = t

            def up(i):
                g, j, b = i // 4, i % 4, i % 2

                def go(e):
                    r = e.value_load(eoff[h][1024][0:1, i:i + 1], min_val=0, max_val=1024 * (E - 1))
                    return e.matmul(HB[b][:], xT[g % 2][:, j * P:(j + 1) * P], W2[:, bass.ds(r, HID)],
                                    start=True, stop=True)
                t = op("pe", go, xT_ready[g % 2], t_w, *tok["eoff"][h], *H_free[b])
                xT_free[g % 2] = [t]

                def bias(e):
                    r = e.value_load(eoff[h][512][0:1, i:i + 1], min_val=0, max_val=512 * (E - 1))
                    return e.tensor_tensor(Hb[b][:], HB[b][:], BU[:, bass.ds(r, HID)], ALU.add)
                t = op("dve", bias, t, t_w, *tok["eoff"][h], *Hb_free[b])
                H_free[b] = [t]
                t = op("act", lambda e: e.activation(G[b][:], Hb[b][:], ACT.Gelu), t, *G_free[b])
                Hb_free[b] = [t]
                tok[("G", i)] = t

            def turn_h(i):
                b = i % 2

                def go(e):
                    for c in range(4):
                        x = e.transpose(HTB[b][:, c * P:(c + 1) * P], G[b][:, c * P:(c + 1) * P], ident[:])
                    return x
                t = op("pe", go, tok[("G", i)], *HT_free[b])
                G_free[b] = [t]
                t = op("act", lambda e: e.activation(hT[b][:], HTB[b][:], ACT.Copy), t, *hT_free[b])
                HT_free[b] = [t]
                tok[("hT", i)] = t

            def down(i):
                g, j, b = i // 4, i % 4, i % 2

                def go(e):
                    r = e.value_load(eoff[h][1024][0:1, i:i + 1], min_val=0, max_val=1024 * (E - 1))
                    for c in range(4):
                        x = e.matmul(YB[:, j * P:(j + 1) * P], hT[b][:, c * P:(c + 1) * P],
                                     W2[:, bass.ds(r + HID + c * P, P)], start=(c == 0), stop=(c == 3))
                    return x
                t = op("pe", go, tok[("hT", i)], *Y_free)
                hT_free[b] = [t]

                def bias(e):
                    r = e.value_load(eoff[h][128][0:1, i:i + 1], min_val=0, max_val=128 * (E - 1))
                    return e.tensor_tensor(Ys[g % 2][:, j, :], YB[:, j * P:(j + 1) * P], BD[:, bass.ds(r, D)], ALU.add)
                t = op("dve", bias, t, *Ys_free[g % 2])
                Y_free[:] = [t]
                n = size(g)
                if j == n - 1:
                    s = dma("sp", lambda e: e.dma_start(ysv[:, 4 * g:4 * g + n, :], Ys[g % 2][:, 0:n, :]),
                            s_ys[g % 2], t, *tok.get(("yg", h), []))
                    Ys_free[g % 2] = [s]

            load(0)
            for i in range(NTL + 2):
                if i < NTL:
                    if i % 4 == 0:
                        if i == 0:
                            turn_x(0)
                            load(1)
                    up(i)
                    if i % 4 == 2 and i // 4 + 1 < NG:
                        turn_x(i // 4 + 1)
                        if i // 4 + 2 < NG:
                            load(i // 4 + 2)
                if 1 <= i <= NTL:
                    turn_h(i - 1)
                if i >= 2:
                    down(i - 2)
                yield
            tok[("ys", h)] = [Ys_free[0][0], Ys_free[1][0]]
            tok[("xl", h)] = [xl_free[0][0], xl_free[1][0]]

        yg_free = [[] for _ in range(NYG)]
        yg_n = [0]

        def gather(h):
            for q in range(NQ):
                for k in range(K):
                    for j in range(4):
                        t = 4 * q + j
                        s = yg_n[0] % NYG
                        yg_n[0] += 1
                        tg_ = dma("pool", lambda e, t=t, k=k, s=s: e.indirect_dma_start(
                            YG[:, s, :], None, ys[h], bass.IndirectOffsetOnAxis(SLU[h][:, k, t:t + 1], 0),
                            bounds_check=NTL * P - 1, oob_is_err=False),
                            s_yg[s], *tok[("ys", h)], *yg_free[s])
                        g = h * NQ + q
                        before = tok[("sum", g, k - 1, j)] if k else (tok["X"].get(g, [t_x[g]])[0])
                        tok[("sum", g, k, j)] = ts = op("dve", lambda e, t=t, k=k, s=s: e.scalar_tensor_tensor(
                            X[:, h * NT + t, :], YG[:, s, :], WK[h][:, t, k:k + 1], X[:, h * NT + t, :],
                            ALU.mult, ALU.add), tg_, before, *tok["WK"][h])
                        yg_free[s] = [ts]
                tok["X"][h * NQ + q] = [ts]
                tok[("yg", h)] = [tg_]
                tok["SLU"][h] = tok["SLU"][h] + [tg_]
                yield q

        def attn(g):
            tX = tok["X"][g]
            Xq = [X[:, 4 * g + j, :] for j in range(4)]
            xrq = [xr[:, j, :] for j in range(4)]
            t = norm_rows(Xq, xrq, 1e-5, tX, tok["xr"])
            yield
            b, ps, t = turn4(xrq, [t])
            tok["xr"] = [t]
            tx = op("act", lambda e, ps=ps: e.activation(sT[:], ps[:], ACT.Copy), t, *tok["sT"])
            bank_free[b] = [tx]
            yield

            def gated(wa, ba, bah, wb, bb, ready):
                b, ps, t = side_mm(wat[wa], sT, ready)
                op("act", lambda e: e.activation(tg[:], ps[:], ACT.Tanh, bias=bah[:, 0:1], scale=0.5), t, *tok["att"])
                ta = op("act", lambda e: e.activation(ag[:], ps[:], ACT.Identity, bias=vec[ba][:, 0:1]))
                bank_free[b] = [ta]
                b2, ps2, t2 = side_mm(wat[wb], sT, ready)
                tok["sT"] = [t2]
                yield
                t = op("dve", lambda e: e.scalar_tensor_tensor(bu[:], ps2[:], vec[bb][:, 0:1], ag[:], ALU.add, ALU.mult),
                       t2, ta)
                bank_free[b2] = [t]
                tok["u2"] = op("dve", lambda e: e.scalar_tensor_tensor(u2[:], tg[:], 1.0, bu[:], ALU.add, ALU.mult),
                               t, *tok["att"])
                yield

            yield from gated("Wg", "bg", bgh, "Wi", "bi", [tx, t_v, t_acst])
            t = op("dve", lambda e: e.tensor_tensor_scan(sc[:], Arep[:], u2[:], 0.0, ALU.mult, ALU.add), tok["u2"])
            tw = op("act", lambda e: e.activation(wv[:], u2[:], ACT.Copy, scale=cD[:, 0:1]), tok["u2"], *tok["att"])
            t = op("dve", lambda e: e.scalar_tensor_tensor(yv[:], sc[:], cB[:, 0:1], wv[:], ALU.mult, ALU.add), t, tw)
            yield
            b, ps, t = turn4([yv[:, j * P:(j + 1) * P] for j in range(4)], [t])
            t = norm_rows([ps[:, j * P:(j + 1) * P] for j in range(4)], xrq, 1e-3, [t], tok["xr"])
            bank_free[b] = [t]
            yield
            b, ps, t = turn4(xrq, [t])
            tok["xr"] = [t]
            tx = op("act", lambda e, ps=ps: e.activation(sT[:], ps[:], ACT.Identity, bias=vec["beta"][:, 0:1],
                                                         scale=vec["gamma"][:, 0:1]), t, *tok["sT"])
            bank_free[b] = [tx]
            yield
            tok["att"] = [t, tw]
            yield from gated("Wfg", "bfg", bfgh, "Wfu", "bfu", [tx])
            b, ps, t = side_mm(wat["Wfd"], u2, [tok["u2"]])
            tok["att"] = [t]
            to = op("act", lambda e, ps=ps: e.activation(sT[:], ps[:], ACT.Identity, bias=vec["bfd"][:, 0:1], scale=0.5),
                    t, *tok["sT"])
            bank_free[b] = [to]
            yield
            b, ps, free = bank()

            def outp(e):
                for j in range(4):
                    i = e.matmul(ps[:, j * P:(j + 1) * P], sT[:, j * P:(j + 1) * P], wat["Wo"][:], start=True, stop=True)
                return i
            t = op("pe", outp, to, *free)
            tok["sT"] = [t]
            Xf = X[:, 4 * g:4 * g + 4, :]
            t = op("dve", lambda e: e.tensor_tensor(
                xr[:], ps[:, :].rearrange("p (t d) -> p t d", d=D),
                boB[:, :].rearrange("p (o d) -> p o d", o=1).to_broadcast([P, 4, D]), ALU.add), t, *tok["xr"])
            bank_free[b] = [t]
            t = op("dve", lambda e: e.tensor_tensor(Xf, Xf, xr[:], ALU.add), t)
            tok["X"][g] = [t]
            tok["xr"] = [t]
            yield

        def side(h):
            for q in gather(h):
                yield
                yield from attn(h * NQ + q)
                yield from route_quad(h, q)
            yield from route_tail(h)
            scatter(h)

        def final(h):
            for q in gather(h):
                g = h * NQ + q
                tok["out"] = dma("sp", lambda e, g=g: e.dma_start(ov[:, 4 * g:4 * g + 4, :], X[:, 4 * g:4 * g + 4, :]),
                                 s_out, *[tok[("sum", g, K - 1, j)] for j in range(4)])
                yield

        def run(*gens):
            gens = list(gens)
            while gens:
                for x in list(gens):
                    if next(x, gens) is gens:
                        gens.remove(x)

        for h in range(NH):
            for q in range(NQ):
                run(route_quad(h, q))
            run(route_tail(h))
            scatter(h)
            if h == 0:
                t_acst = attn_consts()
        run(ffn(0))
        run(ffn(1), side(0))
        run(ffn(0), side(1))
        run(ffn(1), final(0))
        run(final(1))
        Q.wait("sp", tok["out"])

        block = ctx.enter_context(nc.Block())

        @block.sync
        def _(e):
            Q.emit("sp", e)

        @block.tensor
        def _(e):
            Q.emit("pe", e)

        @block.vector
        def _(e):
            Q.emit("dve", e)

        @block.scalar
        def _(e):
            Q.emit("act", e)

        @block.gpsimd
        def _(e):
            Q.emit("pool", e)


_ATTN = ["Wg", "bg", "Wi", "bi", "A", "Bp", "Cp", "Dp", "gamma", "beta", "Wfg", "bfg", "Wfu", "bfu", "Wfd", "bfd",
         "Wo", "bo"]
_INS = ["L0_attn_x"] + [f"L0_attn_{n}" for n in _ATTN] + [f"L0_ffn_{n}" for n in ("Wg", "Wup", "bup", "Wdown", "bdown")]


def kernel(**inputs):
    import numpy as _np
    import concourse.bacc as _bacc
    from concourse import mybir as _mybir
    from concourse.bass_utils import run_bass_kernel_spmd as _run

    nc = _bacc.Bacc("TRN2", target_bir_lowering=False, num_devices=1)
    arrays, args = {}, {}
    for name in _INS:
        x = _np.ascontiguousarray(inputs[name])
        arrays[f"in_{name}_dram"] = x
        key = "x" if name == "L0_attn_x" else name[3:]
        args[key] = nc.dram_tensor(f"in_{name}_dram", x.shape, _mybir.dt.from_np(x.dtype), kind="ExternalInput").ap()
    out = nc.dram_tensor("out_0_dram", (8, 512, 128), _mybir.dt.float32, kind="ExternalOutput").ap()
    macaron_kernel(nc, args, out)
    r = _run(nc, [arrays], core_ids=[0])
    return r.results[0]["out_0_dram"]
```

```python
from contextlib import ExitStack

import concourse.bass as bass
from concourse import mybir

F32 = mybir.dt.float32
BF16 = mybir.dt.bfloat16
F32R = mybir.dt.float32r
U32 = mybir.dt.uint32
I32 = mybir.dt.int32
ALU = mybir.AluOpType
ACT = mybir.ActivationFunctionType
AX = mybir.AxisListType

P = 128
D = 128
HID = 512
E = 12
K = 3
T = 4096
NH = 2
NT = T // P // NH
NQ = NT // 4
NTL = (K * NT * P + E * (P - 1)) // P
NG = (NTL + 3) // 4
CAP = NT * P + P
NC = 3
NYG = 12
NB = 3
START = 7
STRIDE = 7
RSQRT_SEED = float(0x5F3759DF)


class Queues:

    def __init__(self, sems):
        self.sem = sems
        self.q = {e: [] for e in sems}
        self.n = {e: 0 for e in sems}
        self.landed = {}

    def op(self, e, fn, *waits):
        self.n[e] += 1
        self.q[e].append((waits, fn, self.sem[e], 1))
        return self.sem[e], self.n[e]

    def dma(self, e, fn, sem, *waits):
        self.landed[sem.name] = self.landed.get(sem.name, 0) + 16
        self.q[e].append((waits, fn, sem, 16))
        return sem, self.landed[sem.name]

    def do(self, e, fn, *waits):
        self.q[e].append((waits, fn, None, 0))

    def wait(self, e, *waits):
        self.q[e].append((waits, None, None, 0))

    def emit(self, e, eng):
        seen = {}
        for waits, fn, sem, by in self.q[e]:
            for s, v in waits:
                if seen.get(s.name, 0) < v:
                    eng.wait_ge(s, v)
                    seen[s.name] = v
            if fn is not None:
                i = fn(eng)
                if sem is not None:
                    i.then_inc(sem, by)


def macaron_kernel(nc, a, out):
    with ExitStack() as ctx:
        def sb(name, shape, dt=F32):
            return ctx.enter_context(nc.sbuf_tensor(name, shape, dt))

        def sem(name):
            return ctx.enter_context(nc.semaphore(name))

        psum = [ctx.enter_context(nc.psum_tensor(f"ps{i}", [P, 512], F32)) for i in range(8)]

        xs = [nc.dram_tensor(f"xs{h}", [E * CAP, D], F32, kind="Internal").ap() for h in range(NH)]
        ys = [nc.dram_tensor(f"ys{h}", [NTL * P, D], F32, kind="Internal").ap() for h in range(NH)]

        WH, WL = sb("WH", [P, E, HID], F32R), sb("WL", [P, E, HID], F32R)
        WD = sb("WD", [P, E, HID])
        B3, D3 = sb("B3", [3, E, HID], BF16), sb("D3", [3, E, D], BF16)
        one3 = sb("one3", [3, P], BF16)
        X = sb("X", [P, NH * NT, D])
        XN = [sb(f"XN{h}", [P, NT, D]) for h in range(NH)]
        wgate = sb("wgate", [P, E])
        wat = {n: sb("w_" + n, [P, D]) for n in ("Wg", "Wi", "Wfg", "Wfu", "Wfd", "Wo")}
        vec = {n: sb("v_" + n, [P, 1]) for n in
               ("bg", "bi", "A", "Bp", "Cp", "Dp", "gamma", "beta", "bfg", "bfu", "bfd")}
        bgh, bfgh, cB, cD, bc = (sb(n, [P, 1]) for n in ("bgh", "bfgh", "cB", "cD", "bc"))
        boB = sb("boB", [P, D])
        Arep = sb("Arep", [P, 512])
        ident = sb("ident", [P, P])
        LT = sb("LT", [P, P], BF16)
        ones = sb("ones", [P, P], BF16)
        io12i, io12 = sb("io12i", [P, E], I32), sb("io12", [P, E])
        capi, cap = sb("capi", [P, E], I32), sb("cap", [P, E])
        ioci, ioc = sb("ioci", [P, NT], I32), sb("ioc", [P, NT])
        iotli, iotl = sb("iotli", [1, NTL], I32), sb("iotl", [1, NTL])
        one12 = sb("one12", [P, E])
        zero = sb("zero", [P, D])

        class Chain:
            pass
        chains = []
        for c in range(NC):
            x = Chain()
            x.sT, x.tg, x.ag, x.u2 = (sb(f"{n}{c}", [P, 512]) for n in ("sT", "tg", "ag", "u2"))
            x.st6, x.mv = sb(f"st6{c}", [P, 4, 6]), sb(f"mv{c}", [P, 4, 2])
            x.v1, x.nr, x.na, x.nb = (sb(f"{n}{c}", [P, 4]) for n in ("v1", "nr", "na", "nb"))
            x.L, x.IX, x.IF = sb(f"L{c}", [P, 4, E]), sb(f"IX{c}", [P, 4, 8], U32), sb(f"IF{c}", [P, 4, K])
            x.M01, x.M = sb(f"M01{c}", [P, 4, E]), sb(f"M{c}", [P, 4, E], BF16)
            x.SL2, x.tk = sb(f"SL2{c}", [P, 4, E]), sb(f"tk{c}", [P, K, 4, E])
            x.SLF = sb(f"SLF{c}", [P, K, 4])
            x.done = []
            chains.append(x)

        V = [sb(f"V{h}", [P, NT, 8]) for h in range(NH)]
        dV, eV = sb("dV", [P, NT, K]), sb("eV", [P, NT, K])
        sV, rV = sb("sV", [P, NT]), sb("rV", [P, NT])
        WK = [sb(f"WK{h}", [P, NT, K]) for h in range(NH)]
        OH = [sb(f"OH{h}", [P, K, NT, E], BF16) for h in range(NH)]
        SX = [sb(f"SX{h}", [P, K, NT], U32) for h in range(NH)]
        SXF = [sb(f"SXF{h}", [P, K, NT]) for h in range(NH)]
        SY = [sb(f"SY{h}", [P, K, NT], U32) for h in range(NH)]
        RC = [sb(f"RC{h}", [P, 2, E]) for h in range(NH)]
        cnt, nte, end, base, dlt, enl = (sb(n, [P, E]) for n in ("cnt", "nte", "end", "base", "dlt", "enl"))
        gt = sb("gt", [P, E, NT])
        tky, SYF = sb("tky", [P, K, NT, E]), sb("SYF", [P, K, NT])
        ie, EF, RF = (sb(n, [1, NTL]) for n in ("ie", "EF", "RF"))
        ge, oe = sb("ge", [1, NTL, E]), sb("oe", [1, NTL, E])
        eW = [sb(f"eW{h}", [1, NTL], U32) for h in range(NH)]
        eD = [sb(f"eD{h}", [1, NTL], U32) for h in range(NH)]
        eR = [sb(f"eR{h}", [1, NTL], U32) for h in range(NH)]
        eP = [sb(f"eP{h}", [1, E], U32) for h in range(NH)]

        xl = [sb(f"xl{i}", [P, 4, D]) for i in range(2)]
        xTh = [sb(f"xTh{i}", [P, 512], F32R) for i in range(2)]
        xTl = [sb(f"xTl{i}", [P, 512], F32R) for i in range(2)]
        G = [sb(f"G{i}", [P, 512]) for i in range(NB)]
        hT = [sb(f"hT{i}", [P, 512]) for i in range(NB)]
        Ys = [sb(f"Ys{i}", [P, 4, D]) for i in range(2)]
        YG = sb("YG", [P, NYG, D])

        s_eng = {e: sem("s_" + e) for e in ("pe", "dve", "act", "pool")}
        Q = Queues({**s_eng, "sp": s_eng["pe"]})
        op, dma = Q.op, Q.dma
        s_x = [sem(f"s_x{i}") for i in range(NH * NQ)]
        s_w, s_wg, s_v, s_br, s_b3 = (sem(n) for n in ("s_w", "s_wg", "s_v", "s_br", "s_b3"))
        s_up = [sem(f"s_up{i}") for i in range(6)]
        s_pad = [sem(f"s_pad{h}") for h in range(NH)]
        s_xl = [sem(f"s_xl{i}") for i in range(2)]
        s_ys = [sem(f"s_ys{i}") for i in range(2)]
        s_sc = [sem(f"s_sc{h}") for h in range(NH)]
        s_yg = [sem(f"s_yg{i}") for i in range(NYG)]
        s_out = sem("s_out")

        xv = a["x"].rearrange("b s d -> (b s) d").rearrange("(t p) d -> p t d", p=P)
        ov = out.rearrange("b s d -> (b s) d").rearrange("(t p) d -> p t d", p=P)
        t_x = {}
        for q in range(NH * NQ):
            t_x[q] = dma("sp", lambda e, q=q: e.dma_start(X[:, 4 * q:4 * q + 4, :], xv[:, 4 * q:4 * q + 4, :]), s_x[q])
            if q == 0:
                t_wg = dma("sp", lambda e: e.dma_start(wgate[:], a["ffn_Wg"]), s_wg)
        stage = [G[0], G[1], G[2], hT[0], hT[1], hT[2]]
        yf = YG[:, :, :].rearrange("p s d -> p (s d)")
        br = [yf[0:E, 0:HID + D], yf[0:E, HID + D:2 * (HID + D)], yf[0:E, 0:HID + D]]
        bp = [x[0:E, :].bitcast(BF16)[:, 0:HID + D] for x in (chains[2].tg, chains[2].ag, chains[2].u2)]
        t_br = dma("sp", lambda e: e.dma_start(br[0][:, 0:HID], a["ffn_bup"]), s_br)
        t_br = dma("sp", lambda e: e.dma_start(br[0][:, HID:HID + D], a["ffn_bdown"]), s_br)
        t_up, stage_free = {}, {}

        def load_up(x):
            t_up[x] = dma("sp", lambda e: e.dma_start(stage[x % 6][:], a["ffn_Wup"][x]), s_up[x % 6],
                          *stage_free.get(x - 6, []))

        for x in range(6):
            load_up(x)
        for x in range(E):
            t_w = dma("sp", lambda e, x=x: e.dma_start(
                WD[:, x, :].rearrange("p (c d) -> p c d", d=D),
                a["ffn_Wdown"][x].rearrange("(c p) d -> p c d", p=P)), s_w)
        for n in vec:
            t_v = dma("act", lambda e, n=n: e.dma_start(vec[n][:], a["attn_" + n].rearrange("(p o) -> p o", o=1)), s_v)
        for n in wat:
            t_v = dma("act", lambda e, n=n: e.dma_start(wat[n][:], a["attn_" + n]), s_v)
        t_v = dma("act", lambda e: e.dma_start(boB[:], a["attn_bo"].rearrange("(o d) -> o d", o=1).to_broadcast([P, D])), s_v)

        t = op("pool", lambda e: e.memset(ident[:], 0.0))
        t_id = op("pool", lambda e: e.affine_select(out=ident[:], in_=ident[:], compare_op=ALU.not_equal, fill=1.0,
                                                    base=0, pattern=[[-1, P]], channel_multiplier=1), t)
        op("pool", lambda e: e.iota(io12i[:], [[1, E]], base=0, channel_multiplier=0))
        op("pool", lambda e: e.iota(capi[:], [[CAP, E]], base=0, channel_multiplier=0))
        op("pool", lambda e: e.iota(ioci[:], [[P, NT]], base=0, channel_multiplier=0))
        ti = op("pool", lambda e: e.iota(iotli[:], [[1, NTL]], base=0, channel_multiplier=0))
        t = op("pool", lambda e: e.memset(LT[:], 1.0))
        t = op("pool", lambda e: e.affine_select(out=LT[:], in_=LT[:], compare_op=ALU.is_gt, fill=0.0,
                                                 base=0, pattern=[[1, P]], channel_multiplier=-1), t)
        op("pool", lambda e: e.memset(one3[:], 1.0))
        t_lt = op("pool", lambda e: e.memset(ones[:], 1.0))
        op("dve", lambda e: e.memset(one12[:], 1.0))
        t_zero = op("dve", lambda e: e.memset(zero[:], 0.0))
        op("dve", lambda e: e.tensor_copy(io12[:], io12i[:]), ti)
        op("dve", lambda e: e.tensor_copy(cap[:], capi[:]))
        op("dve", lambda e: e.tensor_copy(ioc[:], ioci[:]))
        t_cst = op("dve", lambda e: e.tensor_copy(iotl[:], iotli[:]))

        def split_weights():
            for x in range(E):
                t = op("act", lambda e, x=x: e.activation(WH[:, x, :], stage[x % 6][:], ACT.Copy), t_up[x])
                t = op("dve", lambda e, x=x: e.tensor_tensor(WL[:, x, :], stage[x % 6][:], WH[:, x, :].bitcast(F32),
                                                             ALU.subtract), t, t_up[x])
                stage_free[x] = [t]
                if x + 6 < E:
                    load_up(x + 6)
            t_split = t
            for n in range(3):
                t = op("dve", lambda e, n=n: e.tensor_copy(bp[n], br[n]), t_br, t)
                if n < 2:
                    t2 = op("dve", lambda e, n=n: e.tensor_tensor(br[n + 1], br[n], bp[n], ALU.subtract), t)
                dma("sp", lambda e, n=n: e.dma_start(B3[n:n + 1, :, :], bp[n][:, 0:HID]), s_b3, t)
                t_b3 = dma("sp", lambda e, n=n: e.dma_start(D3[n:n + 1, :, :], bp[n][:, HID:HID + D]), s_b3, t)
                t = t2
            return t_split, t_b3

        def attn_consts():
            op("dve", lambda e: e.tensor_scalar(bgh[:], vec["bg"][:], 0.5, None, ALU.mult), t_v)
            op("dve", lambda e: e.tensor_scalar(bfgh[:], vec["bfg"][:], 0.5, None, ALU.mult))
            op("dve", lambda e: e.tensor_scalar(cD[:], vec["Dp"][:], 0.5, None, ALU.mult))
            t = op("dve", lambda e: e.tensor_tensor(bc[:], vec["Bp"][:], vec["Cp"][:], ALU.mult))
            op("dve", lambda e: e.tensor_scalar(cB[:], bc[:], 0.5, None, ALU.mult), t)
            t = op("dve", lambda e: e.memset(Arep[:], 0.0))
            return op("dve", lambda e: e.tensor_scalar(Arep[:], Arep[:], vec["A"][:, 0:1], None, ALU.add), t)

        side_banks = psum[5:8]
        bank_free = [[] for _ in side_banks]
        turn = [0]

        def bank():
            b = turn[0] % len(side_banks)
            turn[0] += 1
            return b, side_banks[b], bank_free[b]

        tokX = {g: [t_x[g]] for g in range(NH * NQ)}
        tokSX, tokSY = [[], []], [[], []]
        tokRC, t_tab, t_scat, t_load = [[], []], [None, None], [[], []], [[], []]
        t_ys, t_gat = [[], []], [[], []]
        t_pad = [None, None]

        def norm_rows(c, src, dst, eps, ready, dst_free=()):
            def stats(e):
                for j in range(4):
                    i = e.bn_stats(c.st6[:, j, :], src[j])
                return i

            def aggr(e):
                for j in range(4):
                    i = e.bn_aggr(c.mv[:, j, :], c.st6[:, j, :])
                return i
            t = op("dve", stats, *ready)
            t = op("dve", aggr, t)
            t = op("dve", lambda e: e.tensor_scalar(c.v1[:], c.mv[:, :, 1], eps, None, ALU.add), t)
            t = op("dve", lambda e: e.tensor_scalar(c.na[:].bitcast(U32), c.v1[:].bitcast(U32), 1, None,
                                                    ALU.logical_shift_right), t)
            t = op("dve", lambda e: e.tensor_scalar(c.nr[:].bitcast(I32), c.na[:].bitcast(I32), -1.0, RSQRT_SEED,
                                                    ALU.mult, ALU.add), t)
            for _ in range(3):
                t = op("dve", lambda e: e.tensor_tensor(c.na[:], c.nr[:], c.nr[:], ALU.mult), t)
                t = op("dve", lambda e: e.scalar_tensor_tensor(c.nb[:], c.na[:], -0.5, c.v1[:], ALU.mult, ALU.mult), t)
                t = op("dve", lambda e: e.scalar_tensor_tensor(c.nr[:], c.nb[:], 1.5, c.nr[:], ALU.add, ALU.mult), t)

            def scale(e):
                for j in range(4):
                    i = e.tensor_scalar(dst[j], src[j], c.mv[:, j, 0:1], c.nr[:, j:j + 1], ALU.subtract, ALU.mult)
                return i
            return op("dve", scale, t, *dst_free)

        def turn4(src, ready):
            b, ps, free = bank()

            def go(e):
                for j in range(4):
                    i = e.transpose(ps[:, j * P:(j + 1) * P], src[j], ident[:])
                return i
            return b, ps, op("pe", go, t_id, *ready, *free)

        def side_mm(w, rhs, ready):
            b, ps, free = bank()
            return b, ps, op("pe", lambda e: e.matmul(ps[:], w[:], rhs[:], start=True, stop=True), *ready, *free)

        def route_quad(c, h, q):
            g = h * NQ + q
            dst = [XN[h][:, 4 * q + j, :] for j in range(4)]
            t_xn = norm_rows(c, [X[:, 4 * g + j, :] for j in range(4)], dst, 1e-5, tokX[g] + c.done, t_scat[h])
            yield
            yield
            b, ps, t = turn4(dst, [t_xn])
            tc = op("act", lambda e, ps=ps: e.activation(c.sT[:], ps[:], ACT.Copy), t)
            bank_free[b] = [tc]
            yield
            b, lg, free = bank()

            def logits(e):
                for j in range(4):
                    i = e.matmul(lg[:, j * E:(j + 1) * E], c.sT[:, j * P:(j + 1) * P], wgate[:], start=True, stop=True)
                return i
            t = op("pe", logits, tc, t_wg, *free)
            t = op("dve", lambda e: e.tensor_copy(c.L[:], lg[:, 0:4 * E].rearrange("p (t e) -> p t e", e=E)), t)
            bank_free[b] = [t]

            v = V[h][:, 4 * q:4 * q + 4, :]

            def maxes(e):
                for j in range(4):
                    i = e.max(v[:, j, :], c.L[:, j, :])
                return i

            def idxs(e):
                for j in range(4):
                    i = e.max_index(c.IX[:, j, :], v[:, j, :], c.L[:, j, :])
                return i
            t = op("dve", maxes, t, *tokSY[h])
            t = op("dve", idxs, t)
            t = op("dve", lambda e: e.tensor_copy(c.IF[:], c.IX[:, :, 0:K]), t)
            yield
            oh = [OH[h][:, k, 4 * q:4 * q + 4, :] for k in range(K)]

            def hot(e):
                for k in range(K):
                    i = e.tensor_tensor(oh[k], c.IF[:, :, k:k + 1].to_broadcast([P, 4, E]),
                                        io12[:, :].rearrange("p (o e) -> p o e", o=1).to_broadcast([P, 4, E]),
                                        ALU.is_equal)
                return i
            t = op("dve", hot, t, t_cst, *tokSY[h])
            t = op("dve", lambda e: e.tensor_tensor(c.M01[:], oh[0], oh[1], ALU.add), t)
            t = op("dve", lambda e: e.tensor_tensor(c.M[:], c.M01[:], oh[2], ALU.add), t)
            yield
            yield
            b, ct, free = bank()

            def count(e):
                m = c.M[:, :, :].rearrange("p t e -> p (t e)")
                e.matmul(ct[:, 0:4 * E], LT[:], m, start=True, stop=True)
                for j in range(3):
                    e.matmul(ct[:, (j + 1) * E:4 * E].rearrange("p (t e) -> p t e", e=E), ones[:],
                             c.M[:, j:j + 1, :].to_broadcast([P, 3 - j, E]),
                             start=False, stop=True, skip_group_check=True)
                for j in range(4):
                    i = e.matmul(ct[:, 4 * E:5 * E], ones[:], c.M[:, j, :], start=(j == 0), stop=(j == 3))
                return i
            tp = op("pe", count, t, t_lt, *free)
            yield
            before = cap[:] if q == 0 else RC[h][:, (q - 1) % 2, :]
            t = op("dve", lambda e: e.tensor_tensor(
                c.SL2[:], ct[:, 0:4 * E].rearrange("p (t e) -> p t e", e=E),
                before.rearrange("p (o e) -> p o e", o=1).to_broadcast([P, 4, E]), ALU.add), tp, *tokRC[h])
            tokRC[h] = [op("dve", lambda e: e.tensor_tensor(RC[h][:, q % 2, :], ct[:, 4 * E:5 * E], before, ALU.add),
                           *tokRC[h], *tokSY[h])]
            bank_free[b] = list(tokRC[h])
            t = op("dve", lambda e: e.tensor_tensor(
                c.tk[:, :, :, :].rearrange("p k t e -> p k (t e)"),
                OH[h][:, :, 4 * q:4 * q + 4, :].rearrange("p k t e -> p k (t e)"),
                c.SL2[:, :, :].rearrange("p t e -> p (t e)").rearrange("p (o n) -> p o n", o=1).to_broadcast([P, K, 4 * E]),
                ALU.mult), t)
            t = op("dve", lambda e: e.tensor_reduce(SXF[h][:, :, 4 * q:4 * q + 4], c.tk[:], AX.X, ALU.add), t, *tokSY[h])
            t = op("dve", lambda e: e.tensor_copy(SX[h][:, :, 4 * q:4 * q + 4], SXF[h][:, :, 4 * q:4 * q + 4]), t,
                   *t_scat[h])
            tokSX[h] = [t]
            c.done = [t]
            for j in range(4):
                for k in range(K):
                    x = dma("pool", lambda e, j=j, k=k: e.indirect_dma_start(
                        xs[h], bass.IndirectOffsetOnAxis(SX[h][:, k, 4 * q + j:4 * q + j + 1], 0),
                        XN[h][:, 4 * q + j, :], None, bounds_check=E * CAP - 1, oob_is_err=False),
                        s_sc[h], t, t_xn, *t_load[h])
            if q == NQ - 1:
                t_scat[h] = [x]
            yield

        def route_tail(h):
            last = RC[h][:, (NQ - 1) % 2, :]
            t = op("dve", lambda e: e.tensor_tensor(cnt[:], last, cap[:], ALU.subtract), *tokRC[h])
            op("dve", lambda e: e.tensor_copy(eP[h][:], last[0:1, :]))
            t = op("dve", lambda e: e.tensor_tensor(
                gt[:], cnt[:, :].rearrange("p (e o) -> p e o", o=1).to_broadcast([P, E, NT]),
                ioc[:, :].rearrange("p (o t) -> p o t", o=1).to_broadcast([P, E, NT]), ALU.is_gt), t)
            t = op("dve", lambda e: e.tensor_reduce(nte[:], gt[:], AX.X, ALU.add), t)
            t = op("dve", lambda e: e.tensor_tensor_scan(end[:], one12[:], nte[:], 0.0, ALU.mult, ALU.add), t)
            op("dve", lambda e: e.tensor_scalar(enl[:], end[:], -1.0, None, ALU.add), t)
            t = op("dve", lambda e: e.tensor_tensor(base[:], end[:], nte[:], ALU.subtract), t)
            td = op("dve", lambda e: e.scalar_tensor_tensor(dlt[:], base[:], float(P), cap[:], ALU.mult, ALU.subtract), t)
            t = op("dve", lambda e: e.tensor_scalar(ie[:], iotl[:], enl[0:1, E - 1:E], None, ALU.min), td)
            t = op("dve", lambda e: e.tensor_tensor(
                ge[:], ie[:, :].rearrange("p (i o) -> p i o", o=1).to_broadcast([1, NTL, E]),
                end[0:1, :].rearrange("p (o e) -> p o e", o=1).to_broadcast([1, NTL, E]), ALU.is_ge), t)
            t = op("dve", lambda e: e.tensor_reduce(EF[:], ge[:], AX.X, ALU.add), t)
            op("dve", lambda e: e.tensor_scalar(eW[h][:], EF[:], float(HID), None, ALU.mult), t)
            op("dve", lambda e: e.tensor_scalar(eD[h][:], EF[:], float(D), None, ALU.mult))
            t = op("dve", lambda e: e.tensor_tensor(
                oe[:], EF[:, :].rearrange("p (i o) -> p i o", o=1).to_broadcast([1, NTL, E]),
                io12[0:1, :].rearrange("p (o e) -> p o e", o=1).to_broadcast([1, NTL, E]), ALU.is_equal), t)
            t = op("dve", lambda e: e.tensor_tensor(
                ge[:], oe[:], dlt[0:1, :].rearrange("p (o e) -> p o e", o=1).to_broadcast([1, NTL, E]), ALU.mult), t)
            t = op("dve", lambda e: e.tensor_reduce(RF[:], ge[:], AX.X, ALU.add), t)
            t_tab[h] = op("dve", lambda e: e.scalar_tensor_tensor(eR[h][:], ie[:], float(P), RF[:], ALU.mult, ALU.subtract), t)
            yield
            t = op("dve", lambda e: e.tensor_tensor(
                tky[:, :, :, :].rearrange("p k t e -> p (k t) e"), OH[h][:, :, :, :].rearrange("p k t e -> p (k t) e"),
                dlt[:, :].rearrange("p (o e) -> p o e", o=1).to_broadcast([P, K * NT, E]), ALU.mult), td)
            t2 = op("dve", lambda e: e.tensor_tensor(
                dV[:], V[h][:, :, 0:K], V[h][:, :, 0:1].to_broadcast([P, NT, K]), ALU.subtract))
            t2 = op("act", lambda e: e.activation(eV[:], dV[:], ACT.Exp), t2)
            yield
            t2 = op("dve", lambda e: e.tensor_reduce(sV[:], eV[:], AX.X, ALU.add), t2)
            t2 = op("dve", lambda e: e.reciprocal(rV[:], sV[:]), t2)
            op("dve", lambda e: e.scalar_tensor_tensor(
                WK[h][:], eV[:], 0.5, rV[:, :].rearrange("p (t o) -> p t o", o=1).to_broadcast([P, NT, K]),
                ALU.mult, ALU.mult), t2)
            t = op("dve", lambda e: e.tensor_reduce(SYF[:], tky[:], AX.X, ALU.add), t)
            tokSY[h] = [op("dve", lambda e: e.tensor_tensor(SY[h][:], SYF[:], SXF[h][:], ALU.add), t, *t_gat[h])]

            def pads(e):
                _, v = nc.values_load_multi_w_load_instructions(
                    eP[h][0:1, :], engines=(e.engine,), min_val=0, max_val=E * CAP - P,
                    skip_runtime_bounds_check_because=COUNTS)
                regs[("pad", h)] = v
            Q.do("sp", pads, t_tab[h])
            for x in range(E):
                t_pad[h] = dma("sp", lambda e, x=x: e.dma_start(
                    xs[h][bass.ds(regs[("pad", h)][x], P), :], zero[:]), s_pad[h], t_zero, *t_load[h])
            yield

        COUNTS = "worked out on the chip from counts of at most a half's tokens"
        regs = {}
        xl_free, xT_free, H_free, Ys_free = ([[], []] for _ in range(4))
        G_free, hT_free = ([[] for _ in range(NB)] for _ in range(2))
        XT_free, HT_free, Y_free = [], [], []
        xT_ready = [None, None]
        t_G, t_hT = {}, {}

        def flat(x):
            return x[:, :, :].rearrange("p e n -> p (e n)")

        def ffn(h):
            HB, HTB, XTB, YB = psum[0:2], psum[2], psum[3], psum[4]
            UH, UL, DN, UB, DB = (flat(x) for x in (WH, WL, WD, B3, D3))
            ysv = ys[h].rearrange("(t p) d -> p t d", p=P)
            t_x_in = {}

            def size(g):
                return min(4, NTL - 4 * g)

            def registers(e, name, table, g, top):
                def go(eng):
                    _, v = nc.values_load_multi_w_load_instructions(
                        table[0:1, 4 * g:4 * g + size(g)], engines=(eng.engine,), min_val=0, max_val=top,
                        skip_runtime_bounds_check_because=COUNTS)
                    for j in range(size(g)):
                        regs[(name, 4 * g + j)] = v[j]
                Q.do(e, go, t_tab[h])

            def load(g):
                registers("sp", "row", eR[h], g, E * CAP - P)
                for j in range(size(g)):
                    t_x_in[g] = dma("sp", lambda e, j=j: e.dma_start(
                        xl[g % 2][:, j, :], xs[h][bass.ds(regs[("row", 4 * g + j)], P), :]),
                        s_xl[g % 2], *t_scat[h], t_pad[h], *xl_free[g % 2])

            def turn_x(g):
                n = size(g)

                def go(e):
                    for j in range(n):
                        i = e.transpose(XTB[:, j * P:(j + 1) * P], xl[g % 2][:, j, :], ident[:])
                    return i
                t = op("pe", go, t_x_in[g], *XT_free)
                xl_free[g % 2] = [t]
                t = op("act", lambda e: e.activation(xTh[g % 2][:, 0:n * P], XTB[:, 0:n * P], ACT.Copy), t, *xT_free[g % 2])
                t = op("dve", lambda e: e.tensor_tensor(
                    xTl[g % 2][:, 0:n * P], XTB[:, 0:n * P], xTh[g % 2][:, 0:n * P].bitcast(F32), ALU.subtract), t)
                XT_free[:] = [t]
                xT_ready[g % 2] = t

            def up(i):
                g, j, b = i // 4, i % 4, i % 2
                hi, lo = xTh[g % 2][:, j * P:(j + 1) * P], xTl[g % 2][:, j * P:(j + 1) * P]

                def go(e):
                    r = regs[("w", i)]
                    e.matmul(HB[b][:], hi, UH[:, bass.ds(r, HID)], start=True, stop=False)
                    e.matmul(HB[b][:], hi, UL[:, bass.ds(r, HID)], start=False, stop=False)
                    e.matmul(HB[b][:], lo, UH[:, bass.ds(r, HID)], start=False, stop=False)
                    return e.matmul(HB[b][:], one3[:], UB[:, bass.ds(r, HID)], start=False, stop=True)
                t = op("pe", go, xT_ready[g % 2], t_w, t_split, t_b3, t_lt, *H_free[b])
                xT_free[g % 2] = [t]
                t = op("act", lambda e: e.activation(G[i % NB][:], HB[b][:], ACT.Gelu), t, *G_free[i % NB])
                H_free[b] = [t]
                t_G[i] = t

            def turn_h(i):
                b = i % NB

                def go(e):
                    for c in range(4):
                        x = e.transpose(HTB[:, c * P:(c + 1) * P], G[b][:, c * P:(c + 1) * P], ident[:])
                    return x
                t = op("pe", go, t_G[i], *HT_free)
                G_free[b] = [t]
                t = op("act", lambda e: e.activation(hT[b][:], HTB[:], ACT.Copy), t, *hT_free[b])
                HT_free[:] = [t]
                t_hT[i] = t

            def down(i):
                g, j, b = i // 4, i % 4, i % NB
                n = size(g)

                def go(e):
                    r = regs[("w", i)]
                    for c in range(4):
                        e.matmul(YB[:, 0:P], hT[b][:, c * P:(c + 1) * P], DN[:, bass.ds(r + c * P, P)],
                                 start=(c == 0), stop=False)
                    return e.matmul(YB[:, 0:P], one3[:], DB[:, bass.ds(regs[("d", i)], D)], start=False, stop=True)
                t = op("pe", go, t_hT[i], *Y_free)
                hT_free[b] = [t]
                t = op("act", lambda e: e.activation(Ys[g % 2][:, j, :], YB[:, 0:P], ACT.Copy), t, *Ys_free[g % 2])
                Y_free[:] = [t]
                if j == n - 1:
                    Ys_free[g % 2] = [dma("sp", lambda e: e.dma_start(
                        ysv[:, 4 * g:4 * g + n, :], Ys[g % 2][:, 0:n, :]), s_ys[g % 2], t, *t_gat[h])]

            def group_registers(g):
                registers("pe", "w", eW[h], g, HID * (E - 1))
                registers("pe", "d", eD[h], g, D * (E - 1))

            load(0)
            group_registers(0)
            for i in range(NTL + 4):
                g = i // 4 + 1
                if i < NTL:
                    if i == 0:
                        turn_x(0)
                        load(1)
                    up(i)
                if 2 <= i < NTL + 2:
                    turn_h(i - 2)
                if i >= 4:
                    down(i - 4)
                if i % 4 == 2 and g < NG:
                    turn_x(g)
                    group_registers(g)
                    if g + 1 < NG:
                        load(g + 1)
                yield
            t_ys[h] = [Ys_free[0][0], Ys_free[1][0]]
            t_load[h] = [xl_free[0][0], xl_free[1][0]]

        yg_free = [[] for _ in range(NYG)]
        t_in = {}

        def gather(h, q):
            for k in range(K):
                for j in range(4):
                    s = (12 * q + 4 * k + j) % NYG
                    t_in[(q, k, j)] = dma("pool", lambda e, k=k, j=j, s=s: e.indirect_dma_start(
                        YG[:, s, :], None, ys[h], bass.IndirectOffsetOnAxis(SY[h][:, k, 4 * q + j:4 * q + j + 1], 0),
                        bounds_check=NTL * P - 1, oob_is_err=False), s_yg[s], *t_ys[h], *tokSY[h], *yg_free[s])
            t_gat[h] = [t_in[(q, k, j)] for k in range(K) for j in range(4)]

        def combine(h, q):
            g = h * NQ + q
            ts = tokX[g]
            for k in range(K):
                now = []
                for j in range(4):
                    s = (12 * q + 4 * k + j) % NYG
                    x = op("dve", lambda e, k=k, j=j, s=s: e.scalar_tensor_tensor(
                        X[:, 4 * g + j, :], YG[:, s, :], WK[h][:, 4 * q + j, k:k + 1], X[:, 4 * g + j, :],
                        ALU.mult, ALU.add), t_in[(q, k, j)], *(ts if k == 0 else [ts[j]]))
                    yg_free[s] = [x]
                    now.append(x)
                ts = now
            tokX[g] = ts

        def attn(c, g):
            h, q = g // NQ, g % NQ
            xrq = [XN[h][:, 4 * q + j, :] for j in range(4)]
            t = norm_rows(c, [X[:, 4 * g + j, :] for j in range(4)], xrq, 1e-5, tokX[g] + c.done, t_scat[h])
            yield
            yield
            b, ps, t = turn4(xrq, [t])
            tx = op("act", lambda e, ps=ps: e.activation(c.sT[:], ps[:], ACT.Copy), t)
            bank_free[b] = [tx]
            yield

            def gated(wa, ba, bah, wb, bb, ready):
                b, ps, t = side_mm(wat[wa], c.sT, ready)
                tt = op("act", lambda e: e.activation(c.tg[:], ps[:], ACT.Tanh, bias=bah[:, 0:1], scale=0.5), t)
                ta = op("act", lambda e: e.activation(c.ag[:], ps[:], ACT.Identity, bias=vec[ba][:, 0:1]))
                bank_free[b] = [ta]
                b2, ps2, t2 = side_mm(wat[wb], c.sT, ready)
                yield
                t = op("dve", lambda e: e.scalar_tensor_tensor(c.ag[:], ps2[:], vec[bb][:, 0:1], c.ag[:], ALU.add,
                                                               ALU.mult), t2, ta)
                bank_free[b2] = [t]
                return op("dve", lambda e: e.scalar_tensor_tensor(c.u2[:], c.tg[:], 1.0, c.ag[:], ALU.add, ALU.mult), t, tt)

            tu = yield from gated("Wg", "bg", bgh, "Wi", "bi", [tx, t_v, t_acst])
            tw = op("act", lambda e: e.activation(c.ag[:], c.u2[:], ACT.Copy, scale=cD[:, 0:1]), tu)
            t = op("dve", lambda e: e.tensor_tensor_scan(c.tg[:], Arep[:], c.u2[:], 0.0, ALU.mult, ALU.add), tu)
            t = op("dve", lambda e: e.scalar_tensor_tensor(c.tg[:], c.tg[:], cB[:, 0:1], c.ag[:], ALU.mult, ALU.add), t, tw)
            yield
            yield
            b, ps, t = turn4([c.tg[:, j * P:(j + 1) * P] for j in range(4)], [t])
            yield
            t = norm_rows(c, [ps[:, j * P:(j + 1) * P] for j in range(4)], xrq, 1e-3, [t])
            bank_free[b] = [t]
            yield
            yield
            b, ps, t = turn4(xrq, [t])
            tx = op("act", lambda e, ps=ps: e.activation(c.sT[:], ps[:], ACT.Identity, bias=vec["beta"][:, 0:1],
                                                         scale=vec["gamma"][:, 0:1]), t)
            bank_free[b] = [tx]
            yield
            tu = yield from gated("Wfg", "bfg", bfgh, "Wfu", "bfu", [tx])
            yield
            b, ps, t = side_mm(wat["Wfd"], c.u2, [tu])
            to = op("act", lambda e, ps=ps: e.activation(c.sT[:], ps[:], ACT.Identity, bias=vec["bfd"][:, 0:1], scale=0.5), t)
            bank_free[b] = [to]
            yield
            b, po, free = bank()

            def outp(e):
                for j in range(4):
                    i = e.matmul(po[:, j * P:(j + 1) * P], c.sT[:, j * P:(j + 1) * P], wat["Wo"][:], start=True, stop=True)
                return i
            t = op("pe", outp, to, *free)
            yield
            Xf = X[:, 4 * g:4 * g + 4, :]
            tmp = c.tg[:, :].rearrange("p (t d) -> p t d", d=D)
            t = op("dve", lambda e: e.tensor_tensor(
                tmp, po[:, :].rearrange("p (t d) -> p t d", d=D),
                boB[:, :].rearrange("p (o d) -> p o d", o=1).to_broadcast([P, 4, D]), ALU.add), t)
            bank_free[b] = [t]
            t = op("dve", lambda e: e.tensor_tensor(Xf, Xf, tmp, ALU.add), t)
            tokX[g] = [t]
            c.done = [t]

        def chain(h, q):
            c = chains[q % NC]
            combine(h, q)
            yield
            yield from attn(c, h * NQ + q)
            yield from route_quad(c, h, q)

        def side(h):
            gather(h, 0)
            live, started, n = [], 0, 0
            while started < NQ or live:
                n += 1
                if started < NQ and n >= START + STRIDE * started:
                    live.append(chain(h, started))
                    next(live[-1])
                    started += 1
                    if started < NQ:
                        gather(h, started)
                for x in list(live):
                    if next(x, live) is live:
                        live.remove(x)
                yield
            yield from route_tail(h)

        def first(h):
            for q in range(NQ):
                yield from route_quad(chains[q % NC], h, q)
            yield from route_tail(h)

        def final(h):
            for q in range(NQ):
                gather(h, q)
                combine(h, q)
                g = h * NQ + q
                t_out.append(dma("sp", lambda e, g=g: e.dma_start(ov[:, 4 * g:4 * g + 4, :], X[:, 4 * g:4 * g + 4, :]),
                                 s_out, *tokX[g]))
                for _ in range(START):
                    yield

        def run(*gens):
            gens = list(gens)
            while gens:
                for x in list(gens):
                    if next(x, gens) is gens:
                        gens.remove(x)

        t_out = []
        run(first(0))
        t_split, t_b3 = split_weights()
        t_acst = attn_consts()
        run(ffn(0), first(1))
        run(ffn(1), side(0))
        run(ffn(0), side(1))
        run(ffn(1), final(0))
        run(final(1))
        Q.wait("sp", t_out[-1])

        block = ctx.enter_context(nc.Block())

        @block.sync
        def _(e):
            Q.emit("sp", e)

        @block.tensor
        def _(e):
            Q.emit("pe", e)

        @block.vector
        def _(e):
            Q.emit("dve", e)

        @block.scalar
        def _(e):
            Q.emit("act", e)

        @block.gpsimd
        def _(e):
            Q.emit("pool", e)


_ATTN = ["Wg", "bg", "Wi", "bi", "A", "Bp", "Cp", "Dp", "gamma", "beta", "Wfg", "bfg", "Wfu", "bfu", "Wfd", "bfd",
         "Wo", "bo"]
_INS = ["L0_attn_x"] + [f"L0_attn_{n}" for n in _ATTN] + [f"L0_ffn_{n}" for n in ("Wg", "Wup", "bup", "Wdown", "bdown")]


def kernel(**inputs):
    import numpy as _np
    import concourse.bacc as _bacc
    from concourse import mybir as _mybir
    from concourse.bass_utils import run_bass_kernel_spmd as _run

    nc = _bacc.Bacc("TRN2", target_bir_lowering=False, num_devices=1)
    arrays, args = {}, {}
    for name in _INS:
        x = _np.ascontiguousarray(inputs[name])
        arrays[f"in_{name}_dram"] = x
        key = "x" if name == "L0_attn_x" else name[3:]
        args[key] = nc.dram_tensor(f"in_{name}_dram", x.shape, _mybir.dt.from_np(x.dtype), kind="ExternalInput").ap()
    out = nc.dram_tensor("out_0_dram", (8, 512, 128), _mybir.dt.float32, kind="ExternalOutput").ap()
    macaron_kernel(nc, args, out)
    r = _run(nc, [arrays], core_ids=[0])
    return r.results[0]["out_0_dram"]
```

```python
from contextlib import ExitStack

import concourse.bass as bass
from concourse import mybir

F32 = mybir.dt.float32
BF16 = mybir.dt.bfloat16
F32R = mybir.dt.float32r
U32 = mybir.dt.uint32
I32 = mybir.dt.int32
ALU = mybir.AluOpType
ACT = mybir.ActivationFunctionType
AX = mybir.AxisListType

P = 128
D = 128
HID = 512
E = 12
ER = E + 1
K = 3
T = 4096
NH = 2
NT = T // P // NH
NQ = NT // 4
NTL = (K * NT * P + E * (P - 1)) // P
NG = (NTL + 3) // 4
CAP = NT * P + P
NC = 4
DX = D + 4
OUTSIDE = 1.0e5
NYS = 4
NB = 2
NGB = 2
ON_ROUTE = "dve"
ON_ATTN = "act"
ON_CONV = "act"
SPARE = -9.0
QUIET = 1.2
SLACK = {"pe": 0.7, "act": 0.1, "dve": 1.8, "sp": 0.0}
LOW = 1.0
LIMIT = 9.0
ACTIVE = 4
PACE = 28.0
AHEAD = 4
RSQRT_SEED = float(0x5F3759DF)


class Queues:

    def __init__(self, sems):
        self.sem = sems
        self.q = {e: [] for e in sems}
        self.n = {e: 0 for e in sems}
        self.landed = {}
        self.clock = {e: 0.0 for e in sems}
        self.at = {}

    def take(self, e, us, waits):
        self.clock[e] = max([self.clock[e]] + [self.at.get((s.name, v), 0.0) + 0.1 for s, v in waits]) + us
        return self.clock[e]

    def op(self, e, fn, *waits, us=0.2):
        self.n[e] += 1
        self.q[e].append((waits, fn, self.sem[e], 1))
        self.at[(self.sem[e].name, self.n[e])] = self.take(e, us, waits)
        return self.sem[e], self.n[e]

    def dma(self, e, fn, sem, *waits):
        self.landed[sem.name] = self.landed.get(sem.name, 0) + 16
        self.q[e].append((waits, fn, sem, 16))
        self.at[(sem.name, self.landed[sem.name])] = self.take(e, 1.04 if e == "pool" else 0.06, waits) + 2.4
        return sem, self.landed[sem.name]

    def ready(self, now, waits):
        return all(self.at[(s.name, v)] <= now for s, v in waits)

    def do(self, e, fn, *waits):
        self.q[e].append((waits, fn, None, 0))

    def wait(self, e, *waits):
        self.q[e].append((waits, None, None, 0))

    def emit(self, e, eng):
        seen = {}
        for waits, fn, sem, by in self.q[e]:
            for s, v in waits:
                if seen.get(s.name, 0) < v:
                    eng.wait_ge(s, v)
                    seen[s.name] = v
            if fn is not None:
                i = fn(eng)
                if sem is not None:
                    i.then_inc(sem, by)


def macaron_kernel(nc, a, out):
    with ExitStack() as ctx:
        def sb(name, shape, dt=F32):
            return ctx.enter_context(nc.sbuf_tensor(name, shape, dt))

        def sem(name):
            return ctx.enter_context(nc.semaphore(name))

        psum = [ctx.enter_context(nc.psum_tensor(f"ps{i}", [P, 512], F32)) for i in range(8)]

        xs = [nc.dram_tensor(f"xs{h}", [E * CAP + P, DX], F32, kind="Internal").ap() for h in range(NH)]
        yk = [nc.dram_tensor(f"yk{h}", [K * NT * P, D], F32, kind="Internal").ap() for h in range(NH)]

        WH, WL = sb("WH", [P, E, HID], F32R), sb("WL", [P, E, HID], F32R)
        WD = sb("WD", [P, E, HID])
        UBR = sb("UBR", [P, E, HID])
        B3 = sb("B3", [3 * ER, HID + D], BF16)
        sel = sb("sel", [3 * ER, ER, P], BF16)
        X = sb("X", [P, NH * NT, D])
        XN = [sb(f"XN{h}", [P, NT, DX]) for h in range(NH)]
        wgate = sb("wgate", [P, E])
        wat = {n: sb("w_" + n, [P, D]) for n in ("Wg", "Wi", "Wfg", "Wfu", "Wfd", "Wo")}
        vec = {n: sb("v_" + n, [P, 1]) for n in
               ("bg", "bi", "A", "Bp", "Cp", "Dp", "gamma", "beta", "bfg", "bfu", "bfd")}
        bgh, bfgh, cB, cD, bc = (sb(n, [P, 1]) for n in ("bgh", "bfgh", "cB", "cD", "bc"))
        ident = sb("ident", [P, P])
        LT = sb("LT", [P, P], BF16)
        ones = sb("ones", [P, P], BF16)
        io12i, io12 = sb("io12i", [P, E], I32), sb("io12", [P, E])
        capi, cap = sb("capi", [P, E], I32), sb("cap", [P, E])
        ioci, ioc = sb("ioci", [P, NT], I32), sb("ioc", [P, NT])
        iotli, iotl = sb("iotli", [P, NTL], I32), sb("iotl", [P, NTL])
        toki = sb("toki", [P, NT], I32)
        gl = sb("gl", [P, 1])
        one12 = sb("one12", [P, E])
        pad = sb("pad", [P, DX])

        class Chain:
            pass
        chains = []
        M01, SL2, tk = sb("M01", [P, 4, E]), sb("SL2", [P, 4, E]), sb("tk", [P, K, 4, E])
        for c in range(NC):
            x = Chain()
            x.sT, x.tg, x.ag = (sb(f"{n}{c}", [P, 512]) for n in ("sT", "tg", "ag"))
            x.st6, x.mv = sb(f"st6{c}", [P, 4, 6]), sb(f"mv{c}", [P, 4, 2])
            x.v1, x.nr, x.na, x.nb = (sb(f"{n}{c}", [P, 4]) for n in ("v1", "nr", "na", "nb"))
            x.IX = sb(f"IX{c}", [P, 4, 8], U32)
            x.OH = sb(f"OH{c}", [P, K, 4, E], BF16)
            x.M01, x.M = M01, sb(f"M{c}", [P, 4, E], BF16)
            x.SL2, x.tk = SL2, tk
            x.SLF = sb(f"SLF{c}", [P, K, 4])
            x.done = []
            chains.append(x)

        V = [sb(f"V{h}", [P, NT, 8]) for h in range(NH)]
        dV, eV = sb("dV", [P, NT, K]), sb("eV", [P, NT, K])
        sV, rV = sb("sV", [P, NT]), sb("rV", [P, NT])
        WK = [sb(f"WK{h}", [P, NT, K]) for h in range(NH)]
        SX = [sb(f"SX{h}", [P, K, NT], U32) for h in range(NH)]
        RC = [sb(f"RC{h}", [P, 2, E]) for h in range(NH)]
        cnt, nte, end, base, dlt, enl = (sb(n, [P, E]) for n in ("cnt", "nte", "end", "base", "dlt", "enl"))
        ie, RF = sb("ie", [P, NTL]), sb("RF", [1, NTL])
        EF = [sb(f"EF{h}", [P, NTL]) for h in range(NH)]
        PEN, RR = sb("PEN", [1, NTL]), sb("RR", [1, NTL])
        eW = [sb(f"eW{h}", [1, NTL], U32) for h in range(NH)]
        eD = [sb(f"eD{h}", [1, NTL], U32) for h in range(NH)]
        eR = [sb(f"eR{h}", [1, NTL], U32) for h in range(NH)]
        eP = [sb(f"eP{h}", [1, E], U32) for h in range(NH)]

        xl = [sb(f"xl{i}", [P, 4, DX]) for i in range(2)]
        xTh = [sb(f"xTh{i}", [P, 512], F32R) for i in range(2)]
        xTl = [sb(f"xTl{i}", [P, 512], F32R) for i in range(2)]
        G = [sb(f"G{i}", [P, 512]) for i in range(NGB)]
        hT = [sb(f"hT{i}", [P, 512]) for i in range(NB)]
        Ys = [sb(f"Ys{i}", [P, 4, D]) for i in range(NYS)]
        eq, dk = sb("eq", [P, 4, 2]), sb("dk", [P, 4])
        row = [sb(f"row{i}", [P, 4], U32) for i in range(NYS + 2)]
        YG = sb("YG", [P, K, 4 * D])
        yf = YG[:, :, :].rearrange("p k n -> p (k n)")
        ge = yf[:, 0:NTL * E].rearrange("p (i e) -> p i e", e=E)
        gt = yf[:, NTL * E:NTL * E + E * NT].rearrange("p (e t) -> p e t", t=NT)

        s_eng = {e: sem("s_" + e) for e in ("pe", "dve", "act", "pool")}
        Q = Queues({**s_eng, "sp": s_eng["pe"]})
        op, dma = Q.op, Q.dma
        s_x = [sem(f"s_x{i}") for i in range(NH * NQ)]
        s_w, s_wg, s_v, s_br, s_b3 = (sem(n) for n in ("s_w", "s_wg", "s_v", "s_br", "s_b3"))
        s_up, s_dn = [sem(f"s_up{i}") for i in range(4)], sem("s_dn")
        s_ub = sem("s_ub")
        s_pad = [sem(f"s_pad{h}") for h in range(NH)]
        s_xl = [sem(f"s_xl{i}") for i in range(2)]
        s_yk = [sem(f"s_yk{i}") for i in range(4 * NYS)]
        s_sc = [sem(f"s_sc{h}") for h in range(NH)]
        s_yg = [sem(f"s_yg{i}") for i in range(12)]
        s_out = sem("s_out")

        xv = a["x"].rearrange("b s d -> (b s) d").rearrange("(t p) d -> p t d", p=P)
        ov = out.rearrange("b s d -> (b s) d").rearrange("(t p) d -> p t d", p=P)
        t_x = {}

        def load_x(q):
            t_x[q] = dma("sp", lambda e: e.dma_start(X[:, 4 * q:4 * q + 4, :], xv[:, 4 * q:4 * q + 4, :]), s_x[q])

        for q in range(NQ):
            load_x(q)
            if q == 0:
                t_wg = dma("sp", lambda e: e.dma_start(wgate[:], a["ffn_Wg"]), s_wg)
        br = [yf[0:ER, 0:HID + D], yf[0:ER, HID + D:2 * (HID + D)], yf[0:ER, 0:HID + D]]
        bp = [x[0:ER, :].bitcast(BF16)[:, 0:HID + D] for x in (chains[1].tg, chains[1].ag, chains[2].tg)]
        t_br = dma("sp", lambda e: e.dma_start(br[0][0:E, 0:HID], a["ffn_bup"]), s_br)
        t_br = dma("sp", lambda e: e.dma_start(br[0][0:E, HID:HID + D], a["ffn_bdown"]), s_br)
        t_br = dma("sp", lambda e: e.dma_start(
            br[0][E:ER, :].rearrange("p (c d) -> p c d", d=D),
            a["attn_bo"].rearrange("(o c d) -> o c d", o=1, c=1).to_broadcast([1, HID // D + 1, D])), s_br)
        t_up = {}
        for x in range(E):
            t_up[x // 3] = dma("sp", lambda e, x=x: e.dma_start(WL[:, x, :].bitcast(F32), a["ffn_Wup"][x]), s_up[x // 3])
        for x in range(E):
            t_dn = dma("sp", lambda e, x=x: e.dma_start(
                WD[:, x, :].rearrange("p (c d) -> p c d", d=D),
                a["ffn_Wdown"][x].rearrange("(c p) d -> p c d", p=P)), s_dn)
        t_ub = dma("sp", lambda e: e.dma_start(
            UBR[:, :, :].rearrange("p e n -> p (e n)"),
            a["ffn_bup"].rearrange("(o e) n -> o (e n)", o=1).to_broadcast([P, E * HID])), s_ub)
        for q in range(NQ, NH * NQ):
            load_x(q)
        for n in vec:
            t_v = dma("sp", lambda e, n=n: e.dma_start(vec[n][:], a["attn_" + n].rearrange("(p o) -> p o", o=1)), s_v)
        for n in wat:
            t_v = dma("sp", lambda e, n=n: e.dma_start(wat[n][:], a["attn_" + n]), s_v)

        t = op("pool", lambda e: e.memset(ident[:], 0.0))
        t_id = op("pool", lambda e: e.affine_select(out=ident[:], in_=ident[:], compare_op=ALU.not_equal, fill=1.0,
                                                    base=0, pattern=[[-1, P]], channel_multiplier=1), t)
        op("pool", lambda e: e.iota(io12i[:], [[1, E]], base=0, channel_multiplier=0))
        op("pool", lambda e: e.iota(capi[:], [[CAP, E]], base=0, channel_multiplier=0))
        op("pool", lambda e: e.iota(ioci[:], [[P, NT]], base=0, channel_multiplier=0))
        op("pool", lambda e: e.iota(iotli[:], [[1, NTL]], base=0, channel_multiplier=0))
        ti = op("pool", lambda e: e.iota(toki[:], [[P, NT]], base=0, channel_multiplier=1))
        t = op("pool", lambda e: e.memset(LT[:], 1.0))
        t = op("pool", lambda e: e.affine_select(out=LT[:], in_=LT[:], compare_op=ALU.is_gt, fill=0.0,
                                                 base=0, pattern=[[1, P]], channel_multiplier=-1), t)
        t = op("pool", lambda e: e.memset(sel[:], 0.0))
        for n in range(3):
            t = op("pool", lambda e, n=n: e.affine_select(
                out=sel[:], in_=sel[:], compare_op=ALU.not_equal, fill=1.0, base=-ER * n, pattern=[[-1, ER], [0, P]],
                channel_multiplier=1), t)
        t_lt = op("pool", lambda e: e.memset(ones[:], 1.0))
        op("dve", lambda e: e.memset(one12[:], 1.0))
        op("dve", lambda e: e.memset(gl[:], 0.0))
        t = op("dve", lambda e: e.memset(pad[:], 0.0))
        t_padrow = op("dve", lambda e: e.memset(pad[:, DX - 1:DX], OUTSIDE), t)
        for h in range(NH):
            op("dve", lambda e, h=h: e.tensor_copy(XN[h][:, :, DX - 1], toki[:]), ti)
        op("dve", lambda e: e.tensor_copy(io12[:], io12i[:]), ti)
        op("dve", lambda e: e.tensor_copy(cap[:], capi[:]))
        op("dve", lambda e: e.tensor_copy(ioc[:], ioci[:]))
        t_cst = op("dve", lambda e: e.tensor_copy(iotl[:], iotli[:]))

        def split_weights():
            for g in range(4):
                hi, lo = WH[:, 3 * g:3 * g + 3, :], WL[:, 3 * g:3 * g + 3, :]
                t = op("act", lambda e, hi=hi, lo=lo: e.activation(hi, lo.bitcast(F32), ACT.Copy), t_up[g])
                t = op("dve", lambda e, hi=hi, lo=lo: e.tensor_tensor(lo, lo.bitcast(F32), hi.bitcast(F32),
                                                                      ALU.subtract), t)
            return t

        def split_biases():
            t = None
            for n in range(3):
                t = op("dve", lambda e, n=n: e.tensor_copy(bp[n], br[n]), t_br, *([t] if t else []))
                t_b3 = dma("sp", lambda e, n=n: e.dma_start(B3[n * ER:n * ER + ER, :], bp[n]), s_b3, t)
                if n < 2:
                    t = op("dve", lambda e, n=n: e.tensor_tensor(br[n + 1], br[n], bp[n], ALU.subtract), t)
            yg_free[0] = yg_free[1] = yg_free[2] = [t]
            return t_b3

        def attn_consts():
            op("dve", lambda e: e.tensor_scalar(bgh[:], vec["bg"][:], 0.5, None, ALU.mult), t_v)
            op("dve", lambda e: e.tensor_scalar(bfgh[:], vec["bfg"][:], 0.5, None, ALU.mult))
            op("dve", lambda e: e.tensor_scalar(cD[:], vec["Dp"][:], 0.5, None, ALU.mult))
            t = op("dve", lambda e: e.tensor_tensor(bc[:], vec["Bp"][:], vec["Cp"][:], ALU.mult))
            return op("dve", lambda e: e.tensor_scalar(cB[:], bc[:], 0.5, None, ALU.mult), t)

        side_banks = psum[5:8]
        bank_free = [[] for _ in side_banks]

        hurry, side_live, tails = [True], [0], [0, 0]

        def room(n=1):
            now = 1e9 if hurry[0] else Q.clock["pe"] + SLACK["pe"]
            return sum(x is not None and Q.ready(now, x) for x in bank_free) >= n

        def bank():
            b = min((b for b in range(len(side_banks)) if bank_free[b] is not None),
                    key=lambda b: max([Q.at[(s.name, v)] for s, v in bank_free[b]] + [0.0]))
            free, bank_free[b] = bank_free[b], None
            return b, side_banks[b], free

        tokX = {g: [t_x[g]] for g in range(NH * NQ)}
        tokWK = [[], []]
        tokRC, t_tab, t_scat, t_load = [[], []], [None, None], [[], []], [[], []]
        t_ys, t_gat = [[], []], [[], []]
        t_pad, routed = [None, None], [0, 0]
        yg_free = [[] for _ in range(4 * K)]

        def norm_rows(c, src, dst, eps, on, ready, dst_free=()):
            def stats(e):
                for j in range(4):
                    i = e.bn_stats(c.st6[:, j, :], src[j])
                return i

            def aggr(e):
                for j in range(4):
                    i = e.bn_aggr(c.mv[:, j, :], c.st6[:, j, :])
                return i
            t = op("dve", stats, *ready, us=0.9)
            t = op("dve", aggr, t, us=0.4)
            yield ("dve",)
            t = op("dve", lambda e: e.tensor_scalar(c.v1[:], c.mv[:, :, 1], eps, None, ALU.add), t)
            t = op("dve", lambda e: e.tensor_scalar(c.nr[:].bitcast(I32), c.v1[:].bitcast(I32), -0.5, RSQRT_SEED,
                                                    ALU.mult, ALU.add), t)
            t = op("dve", lambda e: e.tensor_tensor(c.na[:], c.v1[:], c.nr[:], ALU.mult), t)
            for n in range(3):
                t = op("dve", lambda e: e.scalar_tensor_tensor(c.nb[:], c.na[:], -0.5, c.nr[:], ALU.mult, ALU.mult), t)
                if n < 2:
                    op("dve", lambda e: e.scalar_tensor_tensor(c.na[:], c.nb[:], 1.5, c.na[:], ALU.add, ALU.mult), t, us=0.07)
                t = op("dve", lambda e: e.scalar_tensor_tensor(c.nr[:], c.nb[:], 1.5, c.nr[:], ALU.add, ALU.mult), t)
            if on == "dve":
                def scale(e):
                    for j in range(4):
                        i = e.tensor_scalar(dst[j], src[j], c.mv[:, j, 0:1], c.nr[:, j:j + 1], ALU.subtract, ALU.mult)
                    return i
                return op("dve", scale, t, *dst_free, us=1.1)
            t = op("dve", lambda e: e.scalar_tensor_tensor(c.na[:], c.mv[:, :, 0], -1.0, c.nr[:], ALU.mult, ALU.mult), t)
            yield "act", t

            def scale(e):
                for j in range(4):
                    i = e.activation(dst[j], src[j], ACT.Identity, bias=c.na[:, j:j + 1], scale=c.nr[:, j:j + 1])
                return i
            return op("act", scale, t, *dst_free, us=1.45)

        def turn4(src, ready):
            b, ps, free = bank()

            def go(e):
                for j in range(4):
                    i = e.transpose(ps[:, j * P:(j + 1) * P], src[j], ident[:])
                return i
            return b, ps, op("pe", go, t_id, *ready, *free, us=0.44)

        def side_mm(w, rhs, ready):
            b, ps, free = bank()
            return b, ps, op("pe", lambda e: e.matmul(ps[:], w[:], rhs[:], start=True, stop=True), *ready, *free, us=0.86)

        def route_quad(c, h, q):
            g = h * NQ + q
            dst = [XN[h][:, 4 * q + j, 0:D] for j in range(4)]
            t_xn = yield from norm_rows(c, [X[:, 4 * g + j, :] for j in range(4)], dst, 1e-5, ON_ROUTE, tokX[g] + c.done, t_scat[h])
            yield "pe", t_xn
            while not room():
                yield ("pe",)
            b, ps, t = turn4(dst, [t_xn])
            yield "act", t
            tc = op("act", lambda e, ps=ps: e.activation(c.sT[:], ps[:], ACT.Copy), t, us=0.48)
            bank_free[b] = [tc]
            yield "pe", tc
            while not room():
                yield ("pe",)
            b, lg, free = bank()

            def logits(e):
                for j in range(4):
                    i = e.matmul(lg[:, j * E:(j + 1) * E], c.sT[:, j * P:(j + 1) * P], wgate[:], start=True, stop=True)
                return i
            t = op("pe", logits, tc, t_wg, *free, us=0.3)
            yield "dve", t
            v = V[h][:, 4 * q:4 * q + 4, :]

            def maxes(e):
                for j in range(4):
                    i = e.max(v[:, j, :], lg[:, j * E:(j + 1) * E])
                return i

            def idxs(e):
                for j in range(4):
                    i = e.max_index(c.IX[:, j, :], v[:, j, :], lg[:, j * E:(j + 1) * E])
                return i
            t = op("dve", maxes, t, *tokWK[h], us=0.4)
            t = op("dve", idxs, t, us=0.4)
            bank_free[b] = [t]
            who = XN[h][:, 4 * q:4 * q + 4, D:D + K]
            t = t_who = op("dve", lambda e: e.tensor_copy(who, c.IX[:, :, 0:K]), t)
            oh = [c.OH[:, k, :, :] for k in range(K)]

            def hot(e):
                for k in range(K):
                    i = e.tensor_tensor(oh[k], who[:, :, k:k + 1].to_broadcast([P, 4, E]),
                                        io12[:, :].rearrange("p (o e) -> p o e", o=1).to_broadcast([P, 4, E]),
                                        ALU.is_equal)
                return i
            t = op("dve", hot, t, t_cst, *tokWK[h], us=0.4)
            t = op("dve", lambda e: e.tensor_tensor(c.M01[:], oh[0], oh[1], ALU.add), t)
            t = op("dve", lambda e: e.tensor_tensor(c.M[:], c.M01[:], oh[2], ALU.add), t)
            yield "pe", t
            while not room() or (q and routed[h] != q):
                yield ("pe",)
            routed[h] = q + 1
            b, ct, free = bank()

            def count(e):
                m = c.M[:, :, :].rearrange("p t e -> p (t e)")
                e.matmul(ct[:, 0:4 * E], LT[:], m, start=True, stop=True)
                for j in range(3):
                    e.matmul(ct[:, (j + 1) * E:4 * E].rearrange("p (t e) -> p t e", e=E), ones[:],
                             c.M[:, j:j + 1, :].to_broadcast([P, 3 - j, E]),
                             start=False, stop=True, skip_group_check=True)
                for j in range(4):
                    i = e.matmul(ct[:, 4 * E:5 * E], ones[:], c.M[:, j, :], start=(j == 0), stop=(j == 3))
                return i
            tp = op("pe", count, t, t_lt, *free, us=0.3)
            yield "dve", tp
            before = cap[:] if q == 0 else RC[h][:, (q - 1) % 2, :]
            t = op("dve", lambda e: e.tensor_tensor(
                c.SL2[:], ct[:, 0:4 * E].rearrange("p (t e) -> p t e", e=E),
                before.rearrange("p (o e) -> p o e", o=1).to_broadcast([P, 4, E]), ALU.add), tp, *tokRC[h])
            tokRC[h] = [op("dve", lambda e: e.tensor_tensor(RC[h][:, q % 2, :], ct[:, 4 * E:5 * E], before, ALU.add),
                           *tokRC[h], *tokWK[h])]
            bank_free[b] = list(tokRC[h])
            t = op("dve", lambda e: e.tensor_tensor(
                c.tk[:, :, :, :].rearrange("p k t e -> p k (t e)"),
                c.OH[:, :, :, :].rearrange("p k t e -> p k (t e)"),
                c.SL2[:, :, :].rearrange("p t e -> p (t e)").rearrange("p (o n) -> p o n", o=1).to_broadcast([P, K, 4 * E]),
                ALU.mult), t)
            t = op("dve", lambda e: e.tensor_reduce(c.SLF[:], c.tk[:], AX.X, ALU.add), t, *tokWK[h])
            t = op("dve", lambda e: e.tensor_copy(SX[h][:, :, 4 * q:4 * q + 4], c.SLF[:]), t,
                   *t_scat[h])
            c.done = [t]
            for j in range(4):
                for k in range(K):
                    x = dma("pool", lambda e, j=j, k=k: e.indirect_dma_start(
                        xs[h], bass.IndirectOffsetOnAxis(SX[h][:, k, 4 * q + j:4 * q + j + 1], 0),
                        XN[h][:, 4 * q + j, :], None, bounds_check=E * CAP - 1, oob_is_err=False),
                        s_sc[h], t, t_xn, t_who, *t_load[h])
            if q == NQ - 1:
                t_scat[h] = [x]

        def route_tail(h):
            last = RC[h][:, (NQ - 1) % 2, :]
            t = op("dve", lambda e: e.tensor_tensor(cnt[:], last, cap[:], ALU.subtract), *tokRC[h])
            op("dve", lambda e: e.tensor_copy(eP[h][:], last[0:1, :]))
            t = op("dve", lambda e: e.tensor_tensor(
                gt, cnt[:, :].rearrange("p (e o) -> p e o", o=1).to_broadcast([P, E, NT]),
                ioc[:, :].rearrange("p (o t) -> p o t", o=1).to_broadcast([P, E, NT]), ALU.is_gt), t, *yg_free[0], *yg_free[1], us=0.35)
            t = op("dve", lambda e: e.tensor_reduce(nte[:], gt, AX.X, ALU.add), t, us=0.35)
            t = op("dve", lambda e: e.tensor_tensor_scan(end[:], one12[:], nte[:], 0.0, ALU.mult, ALU.add), t)
            op("dve", lambda e: e.tensor_scalar(enl[:], end[:], -1.0, None, ALU.add), t)
            t = op("dve", lambda e: e.tensor_tensor(base[:], end[:], nte[:], ALU.subtract), t)
            td = op("dve", lambda e: e.scalar_tensor_tensor(dlt[:], base[:], float(P), cap[:], ALU.mult, ALU.subtract), t)
            t = op("dve", lambda e: e.tensor_scalar(ie[:], iotl[:], enl[:, E - 1:E], None, ALU.min), td)
            op("dve", lambda e: e.tensor_scalar(PEN[:], iotl[0:1, :], enl[0:1, E - 1:E], OUTSIDE, ALU.is_gt, ALU.mult))
            t = op("dve", lambda e: e.tensor_tensor(
                ge, ie[:, :].rearrange("p (i o) -> p i o", o=1).to_broadcast([P, NTL, E]),
                end[:, :].rearrange("p (o e) -> p o e", o=1).to_broadcast([P, NTL, E]), ALU.is_ge), t, us=0.9)
            t = op("dve", lambda e: e.tensor_reduce(EF[h][:], ge, AX.X, ALU.add), t, us=0.9)
            op("dve", lambda e: e.tensor_scalar(eW[h][:], EF[h][0:1, :], float(HID), None, ALU.mult), t)
            op("dve", lambda e: e.tensor_scalar(eD[h][:], EF[h][0:1, :], float(D), None, ALU.mult))
            t = op("dve", lambda e: e.tensor_tensor(
                ge[0:1], EF[h][0:1, :].rearrange("p (i o) -> p i o", o=1).to_broadcast([1, NTL, E]),
                io12[0:1, :].rearrange("p (o e) -> p o e", o=1).to_broadcast([1, NTL, E]), ALU.is_equal), t, us=0.9)
            t = op("dve", lambda e: e.tensor_tensor(
                ge[0:1], ge[0:1], dlt[0:1, :].rearrange("p (o e) -> p o e", o=1).to_broadcast([1, NTL, E]), ALU.mult), t, us=0.9)
            t = op("dve", lambda e: e.tensor_reduce(RF[:], ge[0:1], AX.X, ALU.add), t, us=0.9)
            yg_free[0] = yg_free[1] = [t]
            t = op("dve", lambda e: e.scalar_tensor_tensor(RR[:], ie[0:1, :], float(P), RF[:], ALU.mult, ALU.subtract), t)
            t = op("dve", lambda e: e.tensor_tensor(RF[:], RR[:], PEN[:], ALU.add), t)
            t_tab[h] = op("dve", lambda e: e.tensor_scalar(eR[h][:], RF[:], float(E * CAP), None, ALU.min), t)
            yield "sp", t_tab[h]

            def pads(e):
                _, v = nc.values_load_multi_w_load_instructions(
                    eP[h][0:1, :], engines=(e.engine,), min_val=0, max_val=E * CAP - P,
                    skip_runtime_bounds_check_because=COUNTS)
                regs[("pad", h)] = v
            Q.do("sp", pads, t_tab[h])
            t_pad[h] = dma("sp", lambda e: e.dma_start(xs[h][E * CAP:E * CAP + P, :], pad[:]), s_pad[h], t_padrow, *t_load[h])
            for x in range(E):
                t_pad[h] = dma("sp", lambda e, x=x: e.dma_start(
                    xs[h][bass.ds(regs[("pad", h)][x], P), :], pad[:]), s_pad[h], t_padrow, *t_load[h])
            tails[h] += 1
            yield ("dve",)
            t2 = op("dve", lambda e: e.tensor_tensor(
                dV[:], V[h][:, :, 0:K], V[h][:, :, 0:1].to_broadcast([P, NT, K]), ALU.subtract))
            yield "act", t2
            t2 = op("act", lambda e: e.activation(eV[:], dV[:], ACT.Exp), t2, us=1.5)
            op("act", lambda e: e.activation(gl[:], gl[:], ACT.Gelu), t_cst, us=1.5)
            yield "dve", t2
            t2 = op("dve", lambda e: e.tensor_reduce(sV[:], eV[:], AX.X, ALU.add), t2)
            t2 = op("dve", lambda e: e.reciprocal(rV[:], sV[:]), t2)
            tokWK[h] = [op("dve", lambda e: e.scalar_tensor_tensor(
                WK[h][:], eV[:], 0.5, rV[:, :].rearrange("p (t o) -> p t o", o=1).to_broadcast([P, NT, K]),
                ALU.mult, ALU.mult), t2)]

        COUNTS = "worked out on the chip from counts of at most a half's tokens"
        regs = {}
        xl_free, xT_free, H_free = ([[], []] for _ in range(3))
        Ys_free = [[] for _ in range(4 * NYS)]
        row_free = [[] for _ in row]
        t_row, passes = {}, [0, 0]
        G_free, hT_free = [[] for _ in range(NGB)], [[] for _ in range(NB)]
        XT_free, HT_free, Y_free = [], [], []
        xT_ready = [None, None]
        t_G, t_hT = {}, {}

        def flat(x):
            return x[:, :, :].rearrange("p e n -> p (e n)")

        def ffn(halves):
            HB, HTB, XTB, YB = psum[0:2], psum[2], psum[3], psum[4]
            UH, UL, DN, SEL, UB = (flat(x) for x in (WH, WL, WD, sel, UBR))
            t_x_in, behind = {}, []
            groups = [(n, h, g) for n, h in enumerate(halves) for g in range(NG)]
            tiles = [(m, h, 4 * g + j) for m, (n, h, g) in enumerate(groups) for j in range(min(4, NTL - 4 * g))]

            def size(g):
                return min(4, NTL - 4 * g)

            def registers(e, name, table, m, top):
                n, h, g = groups[m]

                def go(eng):
                    _, v = nc.values_load_multi_w_load_instructions(
                        table[h][0:1, 4 * g:4 * g + size(g)], engines=(eng.engine,), min_val=0, max_val=top,
                        skip_runtime_bounds_check_because=COUNTS)
                    for j in range(size(g)):
                        regs[(name, m, j)] = v[j]
                Q.do(e, go, t_tab[h])

            def load(m):
                n, h, g = groups[m]
                registers("sp", "row", eR, m, E * CAP)
                for j in range(size(g)):
                    t_x_in[m] = dma("sp", lambda e, j=j: e.dma_start(
                        xl[m % 2][:, j, :], xs[h][bass.ds(regs[("row", m, j)], P), :]),
                        s_xl[m % 2], *t_scat[h], t_pad[h], *xl_free[m % 2])

            def turn_x(m):
                n, h, g = groups[m]
                w = size(g) * P

                def go(e):
                    for j in range(size(g)):
                        i = e.transpose(XTB[:, j * P:(j + 1) * P], xl[m % 2][:, j, 0:D], ident[:])
                    return i
                t = op("pe", go, t_x_in[m], *XT_free, us=0.44)
                xl_free[m % 2] = [t]
                if g == NG - 1:
                    t_load[h] = [t]
                k = size(g)
                t_r = op("dve", lambda e: e.tensor_tensor(
                    eq[:, 0:k, :], xl[m % 2][:, 0:k, D + 1:D + K],
                    EF[h][:, 4 * g:4 * g + k].rearrange("p (j o) -> p j o", o=1).to_broadcast([P, k, 2]),
                    ALU.is_equal), t_x_in[m], t_tab[h])
                t_r = op("dve", lambda e: e.scalar_tensor_tensor(dk[:, 0:k], eq[:, 0:k, 1], 2.0, eq[:, 0:k, 0],
                                                                 ALU.mult, ALU.add), t_r)
                t_row[m] = op("dve", lambda e: e.scalar_tensor_tensor(
                    row[m % len(row)][:, 0:k], dk[:, 0:k], float(NT * P), xl[m % 2][:, 0:k, DX - 1], ALU.mult, ALU.add),
                    t_r, *row_free[m % len(row)])
                row_free[m % len(row)] = []
                xl_free[m % 2].append(t_row[m])
                t = op("act", lambda e: e.activation(xTh[m % 2][:, 0:w], XTB[:, 0:w], ACT.Copy), t, *xT_free[m % 2], us=0.48)
                t = op("dve", lambda e: e.tensor_tensor(
                    xTl[m % 2][:, 0:w], XTB[:, 0:w], xTh[m % 2][:, 0:w].bitcast(F32), ALU.subtract), t, us=0.6)
                XT_free[:] = [t]
                xT_ready[m % 2] = t
                registers("pe", "w", eW, m, HID * (E - 1))
                registers("pe", "d", eD, m, P * (E - 1))
                registers("dve", "b", eW, m, HID * (E - 1))

            def up(i):
                m, h, k = tiles[i]
                j, b = k % 4, i % 2
                hi, lo = xTh[m % 2][:, j * P:(j + 1) * P], xTl[m % 2][:, j * P:(j + 1) * P]

                def go(e):
                    r = regs[("w", m, j)]
                    e.matmul(HB[b][:], hi, UH[:, bass.ds(r, HID)], start=True, stop=False)
                    e.matmul(HB[b][:], hi, UL[:, bass.ds(r, HID)], start=False, stop=False)
                    x = e.matmul(HB[b][:], lo, UH[:, bass.ds(r, HID)], start=False, stop=aside)
                    if not aside:
                        x = e.matmul(HB[b][:], SEL[:, bass.ds(regs[("d", m, j)], P)], B3[:, 0:HID], start=False, stop=True)
                    return x
                aside = Q.clock["dve"] <= Q.clock["pe"] + (SPARE if side_live[0] else QUIET)
                t = op("pe", go, xT_ready[m % 2], t_split, t_b3[0], t_lt, *H_free[b], us=0.65 if aside else 0.87)
                xT_free[m % 2] = [t]
                if aside:
                    H_free[b] = [op("dve", lambda e: e.tensor_tensor(
                        G[i % NGB][:], HB[b][:], UB[:, bass.ds(regs[("b", m, j)], HID)], ALU.add), t, t_ub,
                        *G_free[i % NGB], us=0.7)]
                    t = op("act", lambda e: e.activation(G[i % NGB][:], G[i % NGB][:], ACT.Gelu), *H_free[b], us=0.48)
                else:
                    t = op("act", lambda e: e.activation(G[i % NGB][:], HB[b][:], ACT.Gelu), t, *G_free[i % NGB], us=0.48)
                    H_free[b] = [t]
                t_G[i] = t

            def turn_h(i):
                b = i % NB

                def go(e):
                    for c in range(4):
                        x = e.transpose(HTB[:, c * P:(c + 1) * P], G[i % NGB][:, c * P:(c + 1) * P], ident[:])
                    return x
                t = op("pe", go, t_G[i], *HT_free, us=0.44)
                G_free[i % NGB] = [t]
                t = op("act", lambda e: e.activation(hT[b][:], HTB[:], ACT.Copy), t, *hT_free[b], us=0.48)
                HT_free[:] = [t]
                t_hT[i] = t

            def down(i):
                m, h, k = tiles[i]
                g, j, b = k // 4, k % 4, i % NB
                n = size(g)

                def go(e):
                    r = regs[("w", m, j)]
                    for c in range(4):
                        e.matmul(YB[:, 0:P], hT[b][:, c * P:(c + 1) * P], DN[:, bass.ds(r + c * P, P)],
                                 start=(c == 0), stop=False)
                    return e.matmul(YB[:, 0:P], SEL[:, bass.ds(regs[("d", m, j)], P)], B3[:, HID:HID + D], start=False, stop=True)
                t = op("pe", go, t_hT[i], t_dn, *Y_free, us=0.93)
                hT_free[b] = [t]
                y = 4 * (m % NYS) + j
                t = op("act", lambda e: e.activation(Ys[m % NYS][:, j, :], YB[:, 0:P], ACT.Copy), t, *Ys_free[y])
                Y_free[:] = [t]
                Ys_free[y] = [dma("pool", lambda e: e.indirect_dma_start(
                    yk[h], bass.IndirectOffsetOnAxis(row[m % len(row)][:, j:j + 1], 0), Ys[m % NYS][:, j, :], None,
                    bounds_check=K * NT * P - 1, oob_is_err=False), s_yk[y], t, t_row[m], *t_gat[h])]
                row_free[m % len(row)] += Ys_free[y]
                if k == NTL - 1:
                    t_ys[h] = sum(Ys_free, [])
                    passes[h] += 1

            load(0)
            turn_x(0)
            load(1)
            for i in range(len(tiles) + 3):
                if 2 <= i < len(tiles) + 2:
                    turn_h(i - 2)
                    yield False
                if i < len(tiles):
                    m, h, k = tiles[i]
                    up(i)
                    yield False
                    if k % 4 == 0:
                        if m + 2 < len(groups):
                            behind.append(m + 2)
                        if m + 1 < len(groups):
                            assert m + 1 not in behind
                            turn_x(m + 1)
                            yield False
                    while behind and tails[groups[behind[0]][1]] > groups[behind[0]][0] // 2:
                        load(behind.pop(0))
                if i >= 3:
                    down(i - 3)
                yield True

        bufs = [YG[:, k, :] for k in range(K)]
        bufs += [x[:, :, :].rearrange("p t n -> p (t n)")[:, k * 512:k * 512 + 512] for x in XN for k in range(K)]
        bufs += [x[:] for x in (chains[0].sT, chains[0].tg, chains[0].ag)]
        bufs = [x.rearrange("p (t d) -> p t d", t=4) for x in bufs]
        t_in = {}

        def load_y(h, q, s, k):
            b = K * s + k
            src = yk[h].rearrange("(k t p) d -> k p t d", k=K, p=P)[k]
            t_in[(h, q, k)] = b, dma("sp", lambda e: e.dma_start(bufs[b], src[:, 4 * q:4 * q + 4, :]),
                                     s_yg[b], *t_ys[h], *yg_free[b])
            t_gat[h] = [t_in[(h, x, y)][1] for x in range(q + 1) for y in range(K) if (h, x, y) in t_in]

        def combine(h, q, reload):
            g = h * NQ + q
            ts = tokX[g]
            for k in range(K):
                b, t = t_in[(h, q, k)]
                now = []
                for j in range(4):
                    now.append(op("dve", lambda e, k=k, j=j, b=b: e.scalar_tensor_tensor(
                        X[:, 4 * g + j, :], bufs[b][:, j, :], WK[h][:, 4 * q + j, k:k + 1], X[:, 4 * g + j, :],
                        ALU.mult, ALU.add), t, *tokWK[h], *(ts if k == 0 else [ts[j]]), us=0.27))
                ts = yg_free[b] = now
                if reload and q + 1 < NQ:
                    load_y(h, q + 1, 0, k)
                yield ("dve",)
            tokX[g] = ts

        def combine_pe(h, q):
            g = h * NQ + q
            b, ps, free = bank()
            Xf = X[:, 4 * g:4 * g + 4, :].rearrange("p t d -> p (t d)")
            op("pe", lambda e: e.matmul(ps[:], ident[:], Xf, start=True, stop=False), t_id, *tokX[g], *free, us=0.86)
            for k in range(K):
                y, t = t_in[(h, q, k)]

                def scale(e, y=y, k=k):
                    for j in range(4):
                        i = e.activation(bufs[y][:, j, :], bufs[y][:, j, :], ACT.Copy, scale=WK[h][:, 4 * q + j, k:k + 1])
                    return i
                t = op("act", scale, t, *tokWK[h], us=0.8)
                t = op("pe", lambda e, y=y, k=k: e.matmul(ps[:], ident[:], bufs[y].rearrange("p t d -> p (t d)"),
                                                          start=False, stop=(k == K - 1)), t, us=0.86)
                yield
            t = op("act", lambda e: e.activation(Xf, ps[:], ACT.Copy), t, us=0.48)
            bank_free[b] = tokX[g] = [t]
            store(g)

        def store(g):
            t_out.append(dma("sp", lambda e: e.dma_start(ov[:, 4 * g:4 * g + 4, :], X[:, 4 * g:4 * g + 4, :]),
                             s_out, *tokX[g]))

        def attn(c, g):
            h, q = g // NQ, g % NQ
            xrq = [XN[h][:, 4 * q + j, 0:D] for j in range(4)]
            t = yield from norm_rows(c, [X[:, 4 * g + j, :] for j in range(4)], xrq, 1e-5, ON_ATTN, tokX[g] + c.done, t_scat[h])
            yield "pe", t
            while not room():
                yield ("pe",)
            b, ps, t = turn4(xrq, [t])
            yield "act", t
            tx = op("act", lambda e, ps=ps: e.activation(c.sT[:], ps[:], ACT.Copy), t, us=0.48)
            bank_free[b] = [tx]
            yield "pe", tx

            def gated(wa, ba, bah, wb, bb, ready):
                while not room(2):
                    yield ("pe",)
                b, ps, t = side_mm(wat[wa], c.sT, ready)
                b2, ps2, t2 = side_mm(wat[wb], c.sT, ready)
                yield "act", t
                tt = op("act", lambda e: e.activation(c.tg[:], ps[:], ACT.Tanh, bias=bah[:, 0:1], scale=0.5), t, us=0.6)
                ta = op("act", lambda e: e.activation(c.ag[:], ps[:], ACT.Identity, bias=vec[ba][:, 0:1]), us=0.6)
                bank_free[b] = [ta]
                yield "dve", t2, ta
                t = op("dve", lambda e: e.scalar_tensor_tensor(c.ag[:], ps2[:], vec[bb][:, 0:1], c.ag[:], ALU.add,
                                                               ALU.mult), t2, ta, us=0.7)
                bank_free[b2] = [t]
                return op("dve", lambda e: e.scalar_tensor_tensor(c.tg[:], c.tg[:], 1.0, c.ag[:], ALU.add, ALU.mult), t, tt,
                          us=0.7)

            tu = yield from gated("Wg", "bg", bgh, "Wi", "bi", [tx, t_v, t_acst])
            t = op("dve", lambda e: e.tensor_tensor_scan(c.sT[:], vec["A"][:, 0:1].to_broadcast([P, 512]), c.tg[:], 0.0,
                                                         ALU.mult, ALU.add), tu, us=0.7)
            yield "act", tu
            tw = op("act", lambda e: e.activation(c.ag[:], c.tg[:], ACT.Copy, scale=cD[:, 0:1]), tu, us=0.65)
            yield "dve", tw
            t = op("dve", lambda e: e.scalar_tensor_tensor(c.sT[:], c.sT[:], cB[:, 0:1], c.ag[:], ALU.mult, ALU.add), t, tw, us=0.7)
            yield "pe", t
            while not room():
                yield ("pe",)
            b, ps, t = turn4([c.sT[:, j * P:(j + 1) * P] for j in range(4)], [t])
            yield "dve", t
            t = yield from norm_rows(c, [ps[:, j * P:(j + 1) * P] for j in range(4)], xrq, 1e-3, ON_CONV, [t])
            bank_free[b] = [t]
            yield "pe", t
            while not room():
                yield ("pe",)
            b, ps, t = turn4(xrq, [t])
            yield "act", t
            tx = op("act", lambda e, ps=ps: e.activation(c.sT[:], ps[:], ACT.Identity, bias=vec["beta"][:, 0:1],
                                                         scale=vec["gamma"][:, 0:1]), t, us=0.66)
            bank_free[b] = [tx]
            yield "pe", tx
            tu = yield from gated("Wfg", "bfg", bfgh, "Wfu", "bfu", [tx])
            yield "pe", tu
            while not room():
                yield ("pe",)
            b, ps, t = side_mm(wat["Wfd"], c.tg, [tu])
            yield "act", t
            to = op("act", lambda e, ps=ps: e.activation(c.sT[:], ps[:], ACT.Identity, bias=vec["bfd"][:, 0:1], scale=0.5), t, us=0.6)
            bank_free[b] = [to]
            yield "pe", to
            while not room():
                yield ("pe",)
            b, po, free = bank()

            def outp(e):
                e.matmul(po[:, :].rearrange("p (t d) -> p t d", d=D), sel[:, E, :],
                         B3[:, HID:HID + D].rearrange("p (o d) -> p o d", o=1).to_broadcast([3 * ER, 4, D]),
                         start=True, stop=True)
                for j in range(4):
                    i = e.matmul(po[:, j * P:(j + 1) * P], c.sT[:, j * P:(j + 1) * P], wat["Wo"][:],
                                 start=False, stop=True, skip_group_check=True)
                return i
            t = op("pe", outp, to, t_b3[0], *free, us=1.09)
            yield "dve", t
            Xf = X[:, 4 * g:4 * g + 4, :]
            t = op("dve", lambda e: e.tensor_tensor(Xf, Xf, po[:, :].rearrange("p (t d) -> p t d", d=D), ALU.add), t, us=0.7)
            bank_free[b] = [t]
            tokX[g] = [t]
            c.done = [t]

        def chain(h, q):
            yield ("dve", *(t_in[(h, q, k)][1] for k in range(K)))
            yield from combine(h, q, True)
            yield from attn(chains[q % NC], h * NQ + q)
            yield from route_quad(chains[q % NC], h, q)

        class Steps:

            def __init__(self):
                self.live = []

            def add(self, gen):
                self.live.append([next(gen), gen])

            def tick(self):
                for n, x in enumerate(list(self.live)):
                    now = Q.clock["pe"]
                    (engine, *waits), gen = x
                    if hurry[0] or (Q.ready(now + SLACK[engine], waits) and
                                    (engine != "dve" or Q.clock["dve"] <= now + (LOW if n else LIMIT))):
                        x[0] = next(gen, None)
                        if x[0] is None:
                            self.live.remove(x)

        def side(h):
            while passes[h] == 0 or not Q.ready(Q.clock["pe"] + 1.0, t_ys[h]):
                yield
            st = Steps()
            for k in range(K):
                load_y(h, 0, 0, k)
            q = 0
            while q < NQ or st.live:
                if q < NQ and (h, q, K - 1) in t_in and len(st.live) < ACTIVE:
                    st.add(chain(h, q))
                    q += 1
                side_live[0] = len(st.live)
                st.tick()
                yield
            side_live[0] = 0
            st.add(route_tail(h))
            while st.live:
                st.tick()
                yield

        def first_alone(h):
            gens = [route_quad(chains[q % NC], h, q) for q in range(NQ)]

            def steps(q, n):
                for _ in range(n):
                    next(gens[q], None)
            n = 3 if ON_ROUTE == "act" else 2
            steps(0, n + 2)
            for q in range(NQ):
                if q + 1 < NQ:
                    steps(q + 1, n)
                steps(q, 5)
                if q + 1 < NQ:
                    steps(q + 1, 2)
            t_b3.append(split_biases())
            run(route_tail(h))

        def first(h):
            st = Steps()
            q, start = 0, Q.clock["pe"]
            while q < NQ or st.live:
                if q < NQ and (hurry[0] or Q.clock["pe"] >= start + PACE * q):
                    st.add(route_quad(chains[q % NC], h, q))
                    q += 1
                st.tick()
                yield
            st.add(route_tail(h))
            while st.live:
                st.tick()
                yield

        def final(h):
            while not hurry[0] and (passes[h] < 2 or not Q.ready(Q.clock["pe"] + 1.0, t_ys[h])):
                yield
            for q in range(NQ):
                for k in range(K):
                    yg_free[K * q + k] = yg_free[K * q + k] + t_scat[0] + t_scat[1] + chains[0].done
                    load_y(h, q, q, k)
            if not hurry[0]:
                for q in range(NQ):
                    while not Q.ready(Q.clock["pe"], [t_in[(h, q, K - 1)][1]]):
                        yield
                    yield from combine(h, q, False)
                    store(h * NQ + q)
                return
            by_pe = combine_pe(h, 0), combine_pe(h, 2)
            for n in (0, 0, 0, 1, 0, 1, 1):
                next(by_pe[n], None)
            yield from combine(h, 1, False)
            store(h * NQ + 1)
            next(by_pe[1], None)
            yield from combine(h, 3, False)
            store(h * NQ + 3)

        def run(gen):
            hurry[0] = True
            for _ in gen:
                pass
            hurry[0] = False

        t_out, t_b3 = [], []
        first_alone(0)
        hurry[0] = False
        t_split = split_weights()
        t_acst = attn_consts()
        main = ffn([0, 1, 0, 1])

        def tile():
            while not next(main, True):
                yield

        works = []
        for n, work in enumerate((first(1), side(0), side(1), final(0))):
            works.append(work)
            for _ in range(NTL - AHEAD):
                for _ in tile():
                    for w in works:
                        next(w, None)
            hurry[0] = True
            while n < 3 and sum(tails) < n + 2:
                next(work)
            hurry[0] = False
            for _ in range(AHEAD):
                for _ in tile():
                    for w in works:
                        next(w, None)
        for w in works:
            run(w)
        run(main)
        run(final(1))
        Q.wait("sp", t_out[-1])

        block = ctx.enter_context(nc.Block())

        @block.sync
        def _(e):
            Q.emit("sp", e)

        @block.tensor
        def _(e):
            Q.emit("pe", e)

        @block.vector
        def _(e):
            Q.emit("dve", e)

        @block.scalar
        def _(e):
            Q.emit("act", e)

        @block.gpsimd
        def _(e):
            Q.emit("pool", e)


_ATTN = ["Wg", "bg", "Wi", "bi", "A", "Bp", "Cp", "Dp", "gamma", "beta", "Wfg", "bfg", "Wfu", "bfu", "Wfd", "bfd",
         "Wo", "bo"]
_INS = ["L0_attn_x"] + [f"L0_attn_{n}" for n in _ATTN] + [f"L0_ffn_{n}" for n in ("Wg", "Wup", "bup", "Wdown", "bdown")]


def kernel(**inputs):
    import numpy as _np
    import concourse.bacc as _bacc
    from concourse import mybir as _mybir
    from concourse.bass_utils import run_bass_kernel_spmd as _run

    nc = _bacc.Bacc("TRN2", target_bir_lowering=False, num_devices=1)
    arrays, args = {}, {}
    for name in _INS:
        x = _np.ascontiguousarray(inputs[name])
        arrays[f"in_{name}_dram"] = x
        key = "x" if name == "L0_attn_x" else name[3:]
        args[key] = nc.dram_tensor(f"in_{name}_dram", x.shape, _mybir.dt.from_np(x.dtype), kind="ExternalInput").ap()
    out = nc.dram_tensor("out_0_dram", (8, 512, 128), _mybir.dt.float32, kind="ExternalOutput").ap()
    macaron_kernel(nc, args, out)
    r = _run(nc, [arrays], core_ids=[0])
    return r.results[0]["out_0_dram"]
```
